# Optimizing a Trainium2 kernel written in Bass

```python
import numpy as np
import jax
import jax.numpy as jnp

def _softmax(x, axis=-1):
    return jax.nn.softmax(x, axis=axis)

def _gelu(x):
    return jax.nn.gelu(x, approximate=True)

def _silu(x):
    return jax.nn.silu(x)

def _sigmoid(x):
    return jax.nn.sigmoid(x)

def _layernorm(x, axis=-1, eps=1e-05):
    m = jnp.mean(x, axis=axis, keepdims=True)
    v = jnp.var(x, axis=axis, keepdims=True)
    return (x - m) / jnp.sqrt(v + eps)

def _scatter_add(tgt, idx, src, axis=0):
    return tgt.at[idx].add(src)

def _segment_sum(src, seg, n):
    return jax.ops.segment_sum(src, seg, n)
kernel_name = 'mk_gnn_preln_d4_gnn_r8_eb46f0'

def setup_inputs(seed: int=0):
    np.random.seed(seed)
    _w = jnp.asarray

    def _rec_inputs():
        import jax
        import jax.numpy as jnp
        _gk = jax.random.key(seed)
        x = -0.0009044 + 1 * jax.random.normal(jax.random.fold_in(_gk, 1), (12500, 32), jnp.float32)
        src = jax.random.randint(jax.random.fold_in(_gk, 2), (400000,), 0, 12500, jnp.int32)
        dst = jax.random.randint(jax.random.fold_in(_gk, 3), (400000,), 0, 12500, jnp.int32)
        _o = jnp.argsort(dst, stable=True)
        src = src[_o]
        dst = dst[_o]
        edge_attr_10 = jax.random.uniform(jax.random.fold_in(_gk, 12), (400000, 10), jnp.float32, 0.0, 1)
        edge_attr_3 = 0.00109039 + 0.999626 * jax.random.normal(jax.random.fold_in(_gk, 13), (400000, 3), jnp.float32)
        edge_attr_32 = -9.77346e-05 + 0.999888 * jax.random.normal(jax.random.fold_in(_gk, 14), (400000, 32), jnp.float32)
        edge_attr_4 = 0.00109026 + 0.999989 * jax.random.normal(jax.random.fold_in(_gk, 15), (400000, 4), jnp.float32)
        edge_attr_8 = jax.random.uniform(jax.random.fold_in(_gk, 16), (400000, 8), jnp.float32, 0.0, 1)
        edge_weight = jax.random.uniform(jax.random.fold_in(_gk, 17), (400000,), jnp.float32, 0.0, 0.999997)
        return (x, src, dst, edge_attr_10, edge_attr_3, edge_attr_32, edge_attr_4, edge_attr_8, edge_weight)
    x, src, dst, edge_attr_10, edge_attr_3, edge_attr_32, edge_attr_4, edge_attr_8, edge_weight = _rec_inputs()

    def _L0_gnn_setup():
        import jax, jax.numpy as jnp
        import numpy as np
        N_NODES = 6250
        N_EDGES = 200000
        D_FEAT = 32
        key = jax.random.key(seed)
        k1, k2, k3, k4 = jax.random.split(key, 4)
        node_feat = jax.random.normal(k1, (N_NODES, D_FEAT), dtype=jnp.float32)
        edge_feat = jax.random.normal(k2, (N_EDGES, D_FEAT), dtype=jnp.float32)
        eps = jnp.zeros((1,), dtype=jnp.float32)
        src = jax.random.randint(k3, (N_EDGES,), 0, N_NODES, dtype=jnp.int64)
        dst = jax.random.randint(k4, (N_EDGES,), 0, N_NODES, dtype=jnp.int64)
        return {'node_feat': node_feat, 'edge_feat': edge_feat, 'eps': eps, 'src': src, 'dst': dst}
    _L0_gnn_all = _L0_gnn_setup()
    _L0_gnn_in = {k: v for k, v in _L0_gnn_all.items() if k in ('eps',)}
    del _L0_gnn_all

    def _L1_gnn_setup():
        import jax, jax.numpy as jnp
        import numpy as np
        MUL = 16
        MOUT = 8
        TANH_GAIN = 1.593
        INV_SQRT3 = 0.5773502691896258
        PW_S = 0.17677669529663687
        PW_V = 0.25

        def _w3j_121():
            s2, s6 = (2 ** 0.5, 6 ** 0.5)
            M = np.zeros((5, 3, 3))
            M[0, 0, 1] = M[0, 1, 0] = 1 / s2
            M[1, 1, 2] = M[1, 2, 1] = 1 / s2
            M[2] = np.diag([-1.0, -1.0, 2.0]) / s6
            M[3, 0, 2] = M[3, 2, 0] = 1 / s2
            M[4] = np.diag([1.0, -1.0, 0.0]) / s2
            return jnp.asarray(np.transpose(M, (1, 0, 2)) / 5 ** 0.5, jnp.float32)
        W3J121 = _w3j_121()

        def _sph(edge_vec):
            n = edge_vec / jnp.linalg.norm(edge_vec, axis=1, keepdims=True)
            x, y, z = (n[:, 0], n[:, 1], n[:, 2])
            y1 = 3.0 ** 0.5 * n
            s15 = 15.0 ** 0.5
            y2 = jnp.stack([s15 * x * y, s15 * y * z, 5.0 ** 0.5 / 2 * (3 * z * z - 1), s15 * x * z, s15 / 2 * (x * x - y * y)], axis=1)
            return (y1, y2)

        def _forward(x, edge_src, edge_dst, edge_vec, emb, norm, W1, W2):
            N, E = (x.shape[0], edge_src.shape[0])
            xs = jnp.concatenate([x[edge_src, :8], x[edge_dst, :8]], axis=1)
            xv = jnp.concatenate([x[edge_src, 8:].reshape(E, 8, 3), x[edge_dst, 8:].reshape(E, 8, 3)], axis=1)
            y1, y2 = _sph(edge_vec)
            h = 2.0 ** 0.5 * jax.nn.relu(emb @ W1 / 10.0 ** 0.5)
            w = (h @ W2 / 16.0 ** 0.5).reshape(E, 7, MUL, MOUT)
            wa_s, wb_s, wa_g, wb_g, wc, wd, we = [w[:, i] for i in range(7)]
            s_out = PW_S * (jnp.einsum('eu,euw->ew', xs, wa_s) + INV_SQRT3 * jnp.einsum('eui,ei,euw->ew', xv, y1, wb_s))
            g_out = PW_S * (jnp.einsum('eu,euw->ew', xs, wa_g) + INV_SQRT3 * jnp.einsum('eui,ei,euw->ew', xv, y1, wb_g))
            v_out = PW_V * (INV_SQRT3 * jnp.einsum('eu,ek,euw->ewk', xs, y1, wc) + INV_SQRT3 * jnp.einsum('eui,euw->ewi', xv, wd) + jnp.einsum('eui,ea,iak,euw->ewk', xv, y2, W3J121, we))
            s_act = TANH_GAIN * jnp.tanh(s_out)
            gates = TANH_GAIN * jnp.tanh(g_out)
            edge_ftr = jnp.concatenate([s_act, (gates[:, :, None] * v_out).reshape(E, 24)], axis=1) * norm[:, None]
            return jax.ops.segment_sum(edge_ftr, edge_dst, num_segments=N)
        key = jax.random.key(seed)
        ks = jax.random.split(key, 8)
        N, E = (6250, 37500)
        return {'x': jax.random.normal(ks[0], (N, 32), jnp.float32), 'edge_src': jax.random.randint(ks[1], (E,), 0, N), 'edge_dst': jax.random.randint(ks[2], (E,), 0, N), 'edge_vec': jax.random.normal(ks[3], (E, 3), jnp.float32), 'emb': jax.random.uniform(ks[4], (E, 10), jnp.float32), 'norm': jax.random.uniform(ks[5], (E,), jnp.float32), 'W1': jax.random.normal(ks[6], (10, 16), jnp.float32), 'W2': jax.random.normal(ks[7], (16, 896), jnp.float32)}
    _L1_gnn_all = _L1_gnn_setup()
    _L1_gnn_in = {k: v for k, v in _L1_gnn_all.items() if k in ('W1', 'W2')}
    del _L1_gnn_all

    def _L2_gnn_setup():
        import jax, jax.numpy as jnp
        import numpy as np
        N_NODES = 12500
        N_EDGES = 200000
        D_FEAT = 32
        key = jax.random.key(seed)
        k1, k2, k3 = jax.random.split(key, 3)
        x = jax.random.normal(k1, (N_NODES, D_FEAT), dtype=jnp.float32)
        edge_row = jax.random.randint(k2, (N_EDGES,), 0, N_NODES, dtype=jnp.int64)
        edge_col = jax.random.randint(k3, (N_EDGES,), 0, N_NODES, dtype=jnp.int64)
        return {'x': x, 'edge_row': edge_row, 'edge_col': edge_col}
    _L2_gnn_all = _L2_gnn_setup()
    _L2_gnn_in = {k: v for k, v in _L2_gnn_all.items() if k in ()}
    del _L2_gnn_all

    def _L3_gnn_setup():
        import jax, jax.numpy as jnp
        import numpy as np
        MUL = 8
        INV_SQRT3 = float(1.0 / np.sqrt(3.0))
        A_SCALAR = float(np.sqrt(1.0 / 128.0))
        A_VECTOR = float(np.sqrt(3.0 / 128.0))
        SQRT2 = float(np.sqrt(2.0))
        N_NODES, N_EDGES, NUM_BASIS, HIDDEN = (6250, 100000, 8, 256)
        WEIGHT_NUMEL = 4 * MUL * MUL
        k = jax.random.split(jax.random.key(seed), 7)
        node_features = jax.random.normal(k[0], (N_NODES, 4 * MUL), jnp.float32)
        edge_src = jax.random.randint(k[1], (N_EDGES,), 0, N_NODES)
        edge_dst = jax.random.randint(k[2], (N_EDGES,), 0, N_NODES)
        edge_sh = jax.random.normal(k[3], (N_EDGES, 4), jnp.float32)
        edge_scalars = jax.random.uniform(k[4], (N_EDGES, NUM_BASIS), jnp.float32)
        fc_w1 = jax.random.normal(k[5], (NUM_BASIS, HIDDEN), jnp.float32)
        fc_w2 = jax.random.normal(k[6], (HIDDEN, WEIGHT_NUMEL), jnp.float32)
        return dict(node_features=node_features, edge_src=edge_src, edge_dst=edge_dst, edge_sh=edge_sh, edge_scalars=edge_scalars, fc_w1=fc_w1, fc_w2=fc_w2)
    _L3_gnn_all = _L3_gnn_setup()
    _L3_gnn_in = {k: v for k, v in _L3_gnn_all.items() if k in ('fc_w1', 'fc_w2')}
    del _L3_gnn_all
    return {'x': x, 'src': src, 'dst': dst, 'edge_attr_10': edge_attr_10, 'edge_attr_3': edge_attr_3, 'edge_attr_32': edge_attr_32, 'edge_attr_4': edge_attr_4, 'edge_attr_8': edge_attr_8, 'edge_weight': edge_weight, 'L0_gnn_eps': _L0_gnn_in['eps'], 'L1_gnn_W1': _L1_gnn_in['W1'], 'L1_gnn_W2': _L1_gnn_in['W2'], 'L3_gnn_fc_w1': _L3_gnn_in['fc_w1'], 'L3_gnn_fc_w2': _L3_gnn_in['fc_w2']}

def reference(x, src, dst, edge_attr_10, edge_attr_3, edge_attr_32, edge_attr_4, edge_attr_8, edge_weight, L0_gnn_eps, L1_gnn_W1, L1_gnn_W2, L3_gnn_fc_w1, L3_gnn_fc_w2):
    import jax
    import jax.numpy as jnp

    def _L0_gnn_ref(node_feat, edge_feat, eps, src, dst):
        import jax, jax.numpy as jnp
        import numpy as np
        N_NODES = 6250
        N_EDGES = 200000
        D_FEAT = 32
        m = jax.nn.relu(node_feat[src] + edge_feat)
        neigh = jax.ops.segment_sum(m, dst, num_segments=node_feat.shape[0])
        return (1.0 + eps[0]) * node_feat + neigh

    def _L1_gnn_ref(x, edge_src, edge_dst, edge_vec, emb, norm, W1, W2):
        import jax, jax.numpy as jnp
        import numpy as np
        MUL = 16
        MOUT = 8
        TANH_GAIN = 1.593
        INV_SQRT3 = 0.5773502691896258
        PW_S = 0.17677669529663687
        PW_V = 0.25

        def _w3j_121():
            s2, s6 = (2 ** 0.5, 6 ** 0.5)
            M = np.zeros((5, 3, 3))
            M[0, 0, 1] = M[0, 1, 0] = 1 / s2
            M[1, 1, 2] = M[1, 2, 1] = 1 / s2
            M[2] = np.diag([-1.0, -1.0, 2.0]) / s6
            M[3, 0, 2] = M[3, 2, 0] = 1 / s2
            M[4] = np.diag([1.0, -1.0, 0.0]) / s2
            return jnp.asarray(np.transpose(M, (1, 0, 2)) / 5 ** 0.5, jnp.float32)
        W3J121 = _w3j_121()

        def _sph(edge_vec):
            n = edge_vec / jnp.linalg.norm(edge_vec, axis=1, keepdims=True)
            x, y, z = (n[:, 0], n[:, 1], n[:, 2])
            y1 = 3.0 ** 0.5 * n
            s15 = 15.0 ** 0.5
            y2 = jnp.stack([s15 * x * y, s15 * y * z, 5.0 ** 0.5 / 2 * (3 * z * z - 1), s15 * x * z, s15 / 2 * (x * x - y * y)], axis=1)
            return (y1, y2)

        def _forward(x, edge_src, edge_dst, edge_vec, emb, norm, W1, W2):
            N, E = (x.shape[0], edge_src.shape[0])
            xs = jnp.concatenate([x[edge_src, :8], x[edge_dst, :8]], axis=1)
            xv = jnp.concatenate([x[edge_src, 8:].reshape(E, 8, 3), x[edge_dst, 8:].reshape(E, 8, 3)], axis=1)
            y1, y2 = _sph(edge_vec)
            h = 2.0 ** 0.5 * jax.nn.relu(emb @ W1 / 10.0 ** 0.5)
            w = (h @ W2 / 16.0 ** 0.5).reshape(E, 7, MUL, MOUT)
            wa_s, wb_s, wa_g, wb_g, wc, wd, we = [w[:, i] for i in range(7)]
            s_out = PW_S * (jnp.einsum('eu,euw->ew', xs, wa_s) + INV_SQRT3 * jnp.einsum('eui,ei,euw->ew', xv, y1, wb_s))
            g_out = PW_S * (jnp.einsum('eu,euw->ew', xs, wa_g) + INV_SQRT3 * jnp.einsum('eui,ei,euw->ew', xv, y1, wb_g))
            v_out = PW_V * (INV_SQRT3 * jnp.einsum('eu,ek,euw->ewk', xs, y1, wc) + INV_SQRT3 * jnp.einsum('eui,euw->ewi', xv, wd) + jnp.einsum('eui,ea,iak,euw->ewk', xv, y2, W3J121, we))
            s_act = TANH_GAIN * jnp.tanh(s_out)
            gates = TANH_GAIN * jnp.tanh(g_out)
            edge_ftr = jnp.concatenate([s_act, (gates[:, :, None] * v_out).reshape(E, 24)], axis=1) * norm[:, None]
            return jax.ops.segment_sum(edge_ftr, edge_dst, num_segments=N)
        return _forward(x, edge_src, edge_dst, edge_vec, emb, norm, W1, W2)

    def _L2_gnn_ref(x, edge_row, edge_col):
        import jax, jax.numpy as jnp
        import numpy as np
        N_NODES = 12500
        N_EDGES = 200000
        D_FEAT = 32
        n = x.shape[0]
        deg = jax.ops.segment_sum(jnp.ones(edge_row.shape[0], dtype=x.dtype), edge_row, num_segments=n)
        norm = jax.lax.rsqrt(1.0 + deg)[:, None]
        xs = norm * x
        agg = jax.ops.segment_sum(xs[edge_col], edge_row, num_segments=n)
        return norm * (agg + xs)

    def _L3_gnn_ref(node_features, edge_src, edge_dst, edge_sh, edge_scalars, fc_w1, fc_w2):
        import jax, jax.numpy as jnp
        import numpy as np
        MUL = 8
        INV_SQRT3 = float(1.0 / np.sqrt(3.0))
        A_SCALAR = float(np.sqrt(1.0 / 128.0))
        A_VECTOR = float(np.sqrt(3.0 / 128.0))
        SQRT2 = float(np.sqrt(2.0))
        N_NODES, N_EDGES, NUM_BASIS, HIDDEN = (6250, 100000, 8, 256)
        WEIGHT_NUMEL = 4 * MUL * MUL
        N = node_features.shape[0]
        E = edge_src.shape[0]
        h = jax.nn.relu(edge_scalars @ (fc_w1 * (1.0 / np.sqrt(NUM_BASIS)))) * SQRT2
        w = (h @ (fc_w2 * (1.0 / np.sqrt(HIDDEN)))).reshape(E, 4, MUL, MUL)
        x = node_features[edge_src]
        s1 = x[:, :MUL]
        v1 = x[:, MUL:].reshape(E, MUL, 3)
        s2 = edge_sh[:, 0]
        v2 = edge_sh[:, 1:4]
        out_s = A_SCALAR * (jnp.einsum('eu,euw->ew', s1 * s2[:, None], w[:, 0]) + INV_SQRT3 * jnp.einsum('eui,ei,euw->ew', v1, v2, w[:, 1]))
        out_v = A_VECTOR * INV_SQRT3 * (jnp.einsum('eu,euw,ei->ewi', s1, w[:, 2], v2) + jnp.einsum('eui,euw->ewi', v1 * s2[:, None, None], w[:, 3]))
        edge_features = jnp.concatenate([out_s, out_v.reshape(E, 3 * MUL)], axis=1)
        node_out = jax.ops.segment_sum(edge_features, edge_dst, num_segments=N)
        return node_out * (1.0 / np.sqrt(E / N))
    h = jnp.maximum(_layernorm(x, axis=-1), 0.0)
    x = x + _L0_gnn_ref(h, edge_attr_32, L0_gnn_eps, src, dst)
    h = jnp.maximum(_layernorm(x, axis=-1), 0.0)
    x = x + _L1_gnn_ref(h, src, dst, edge_attr_3, edge_attr_10, edge_weight, L1_gnn_W1, L1_gnn_W2)
    h = jnp.maximum(_layernorm(x, axis=-1), 0.0)
    x = x + _L2_gnn_ref(h, src, dst)
    h = jnp.maximum(_layernorm(x, axis=-1), 0.0)
    x = x + _L3_gnn_ref(h, src, dst, edge_attr_4, edge_attr_8, L3_gnn_fc_w1, L3_gnn_fc_w2)
    return x

_drawn_inputs = setup_inputs


def setup_inputs(seed=0):
    import zlib

    import numpy as np

    out = dict(_drawn_inputs(seed))
    spreads = {}
    factors = {'edge_attr_4': 8.0, 'edge_attr_8': 8.0, 'L3_gnn_fc_w1': 8.0, 'L3_gnn_fc_w2': 8.0}
    for name, (base, spread) in spreads.items():
        noise = np.random.default_rng([zlib.crc32(name.encode()), seed]).standard_normal(out[name].shape)
        drawn = base * np.exp(spread * noise) if base else spread * noise
        out[name] = jnp.asarray(drawn.astype(out[name].dtype))
    for name, factor in factors.items():
        out[name] = (out[name] * factor).astype(out[name].dtype)
    return out
```

```python
from contextlib import ExitStack

import concourse.bass as bass
from concourse import mybir

F32 = mybir.dt.float32
BF16 = mybir.dt.bfloat16
I32 = mybir.dt.int32
ALU = mybir.AluOpType
ACT = mybir.ActivationFunctionType
AX = mybir.AxisListType

N, D, E = 12500, 32, 400000
P = 128
T = 5
GE = P * T
G = E // GE
NP, NJ = 125, N // 125
EJ = E // NP
UNROLL = 4
PEEL = G - (G - 2 * UNROLL + 3) // UNROLL * UNROLL
TRASH = P
HI = (N + P - 1) // P
MUL1, OUT1, HID1, EMB1 = 16, 8, 16, 10
MUL3, HID3, EMB3 = 8, 256, 8
EPS = 1e-5
TANH_GAIN = 1.593


class Group:

    def __init__(self, base, i=None):
        self.base, self.i = base, i

    def slot(self, n):
        return self.base % n

    def times(self, per, more=0):
        at = per * self.base + more
        return at if self.i is None else self.i * (per * UNROLL) + at

    def turn(self, n):
        at = self.base // n
        return at if self.i is None else self.i * (UNROLL // n) + at


def wait_count(eng, sem, count):
    if isinstance(count, int) and count <= 0:
        return
    eng.wait_ge(sem, count)


def groups(eng, body):
    for g in range(PEEL):
        body(Group(g))
    with eng.Fori(0, (G - PEEL) // UNROLL) as i:
        for c in range(UNROLL):
            body(Group(PEEL + c, i))


assert PEEL >= UNROLL + 1 and (G - PEEL) % UNROLL == 0


def spread(ap, shape, axis):
    return ap.unsqueeze(axis).to_broadcast(shape)


class Sems:

    def __init__(self, nc, ctx, prefix):
        self.nc, self.ctx, self.prefix, self.made = nc, ctx, prefix, {}

    def __call__(self, name):
        if name not in self.made:
            self.made[name] = self.ctx.enter_context(self.nc.semaphore(f"{self.prefix}_{name}"))
        return self.made[name]


def setup_pass(nc, a):
    with ExitStack() as ctx:
        sem = Sems(nc, ctx, "setup")
        sb = lambda name, shape, dt=F32: ctx.enter_context(nc.sbuf_tensor(name, shape, dt))
        zeros = sb("zeros", [P, 4096])
        vec = sb("vec", [NP, EJ * 3])
        square = sb("square", [NP, EJ * 3])
        length = sb("length", [NP, EJ])
        zeroed, x_in, vec_in, lengths, roots, v_step, unit_out, zero_out = (
            sem(n) for n in ("zeroed", "x_in", "vec_in", "lengths", "roots", "v_step", "unit_out", "zero_out"))
        block = ctx.enter_context(nc.Block())

        @block.gpsimd
        def _(pool):
            pool.memset(zeros[:], 0.0).then_inc(zeroed, 1)

        @block.sync
        def _(sp):
            sp.dma_start(vec[:], a["unit_in"]).then_inc(vec_in, 16)
            sp.dma_start(a["x_sb"][:], a["x"]).then_inc(x_in, 16)
            sp.wait_ge(zeroed, 1)
            n = 0
            for table in a["acc"]:
                for t in range(T):
                    rows = table[t]
                    flat = rows[0:N, :].rearrange("(p r) d -> p (r d)", p=NP)
                    sp.dma_start(flat, zeros[0:NP, 0:NJ * D]).then_inc(zero_out, 16)
                    sp.dma_start(rows[N:N + TRASH, :], zeros[0:TRASH, 0:D]).then_inc(zero_out, 16)
                    n += 32
            sp.wait_ge(v_step, 4)
            sp.dma_start(a["unit"], vec[:]).then_inc(unit_out, 16)
            sp.wait_ge(zero_out, n)
            sp.wait_ge(unit_out, 16)
            sp.wait_ge(x_in, 16)

        @block.scalar
        def _(act):
            act.wait_ge(lengths, 1)
            nc.scalar.activation(length[:], length[:], ACT.Sqrt).then_inc(roots, 1)

        @block.vector
        def _(dve):
            v3 = vec[:].rearrange("p (e c) -> p e c", c=3)
            s3 = square[:].rearrange("p (e c) -> p e c", c=3)
            dve.wait_ge(vec_in, 16)
            nc.vector.tensor_mul(square[:], vec[:], vec[:]).then_inc(v_step, 1)
            dve.wait_ge(v_step, 1)
            nc.vector.tensor_reduce(length[:], s3, AX.X, ALU.add).then_inc(lengths, 1)
            dve.wait_ge(roots, 1)
            nc.vector.reciprocal(length[:], length[:]).then_inc(v_step, 1)
            dve.wait_ge(v_step, 2)
            nc.vector.tensor_mul(v3, v3, spread(length[:], [NP, EJ, 3], 2)).then_inc(v_step, 2)


def node_pass(nc, a, layer):
    with ExitStack() as ctx:
        sem = Sems(nc, ctx, f"node{layer}")
        sb = lambda name, shape, dt=F32: ctx.enter_context(nc.sbuf_tensor(f"L{layer}_{name}", shape, dt))
        sums = [sb(f"sums{t}", [NP, NJ * D]) for t in range(T)] if layer else None
        work = sb("work", [NP, NJ * D])
        stat = sb("stat", [NP, NJ])
        deg = sb("deg", [NP, NJ]) if layer == 2 else None
        eps = sb("eps", [NP, 1]) if layer == 1 else None
        sums_in, deg_in, eps_in, v, var_ready, root_ready, deg1_ready, degroot_ready, out_done = (
            sem(n) for n in ("sums_in", "deg_in", "eps_in", "v", "var_ready", "root_ready", "deg1_ready", "degroot_ready", "out_done"))
        x, h, norm = a["x_sb"], a["h_sb"], a["norm_sb"]
        x3, h3, w3 = (z[:].rearrange("p (j d) -> p j d", d=D) for z in (x, h, work))
        block = ctx.enter_context(nc.Block())
        steps = [0]

        @block.sync
        def _(sp):
            if layer:
                for t in range(T):
                    sp.dma_start(sums[t][:], a["acc"][layer - 1][t][0:N, :].rearrange("(p j) d -> p (j d)", p=NP)
                                 ).then_inc(sums_in, 16)
            if layer == 1:
                sp.dma_start(eps[:], a["eps"]).then_inc(eps_in, 16)
            if layer == 2:
                sp.dma_start(deg[:], a["deg"][0:N, :].rearrange("(p j) o -> p (j o)", p=NP)).then_inc(deg_in, 16)

        @block.scalar
        def _(act):
            if layer == 2:
                act.wait_ge(deg1_ready, 1)
                nc.scalar.activation(norm[:], norm[:], ACT.Sqrt).then_inc(degroot_ready, 1)
            if layer < 4:
                act.wait_ge(var_ready, 1)
                nc.scalar.activation(stat[:], stat[:], ACT.Sqrt).then_inc(root_ready, 1)

        @block.vector
        def _(dve):
            def link(ins):
                steps[0] += 1
                ins.then_inc(v, 1)
                dve.wait_ge(v, steps[0])

            if layer:
                dve.wait_ge(sums_in, 16 * T)
                for t in range(1, T):
                    link(nc.vector.tensor_add(sums[0][:], sums[0][:], sums[t][:]))
            if layer == 1:
                dve.wait_ge(eps_in, 16)
                link(nc.vector.tensor_scalar_add(eps[:], eps[:], 1.0))
                link(nc.vector.scalar_tensor_tensor(work[:], h[:], eps[:, 0:1], sums[0][:], ALU.mult, ALU.add))
                link(nc.vector.tensor_add(x[:], x[:], work[:]))
            elif layer == 2:
                link(nc.vector.tensor_add(x[:], x[:], sums[0][:]))
                dve.wait_ge(deg_in, 16)
                nc.vector.tensor_scalar_add(norm[:], deg[:], 1.0).then_inc(deg1_ready, 1)
                dve.wait_ge(degroot_ready, 1)
                link(nc.vector.reciprocal(norm[:], norm[:]))
            elif layer == 3:
                link(nc.vector.tensor_add(work[:], sums[0][:], h[:]))
                link(nc.vector.tensor_mul(w3, w3, spread(norm[:], [NP, NJ, D], 2)))
                link(nc.vector.tensor_add(x[:], x[:], work[:]))
            elif layer == 4:
                link(nc.vector.tensor_add(x[:], x[:], sums[0][:]))
            if layer < 4:
                link(nc.vector.tensor_reduce(stat[:], x3, AX.X, ALU.add))
                link(nc.vector.tensor_scalar_mul(stat[:], stat[:], 1.0 / D))
                link(nc.vector.tensor_tensor(h3, x3, spread(stat[:], [NP, NJ, D], 2), ALU.subtract))
                link(nc.vector.tensor_mul(work[:], h[:], h[:]))
                link(nc.vector.tensor_reduce(stat[:], w3, AX.X, ALU.add))
                nc.vector.tensor_scalar(stat[:], stat[:], 1.0 / D, EPS, ALU.mult, ALU.add).then_inc(var_ready, 1)
                dve.wait_ge(root_ready, 1)
                link(nc.vector.reciprocal(stat[:], stat[:]))
                link(nc.vector.tensor_mul(h3, h3, spread(stat[:], [NP, NJ, D], 2)))
                link(nc.vector.tensor_scalar_max(h[:], h[:], 0.0))
                if layer == 2:
                    link(nc.vector.tensor_mul(h3, h3, spread(norm[:], [NP, NJ, D], 2)))

        @block.gpsimd
        def _(pool):
            pool.wait_ge(v, steps[0])
            out, held = (a["table"][layer], h) if layer < 4 else (a["out"], x)
            pool.dma_start(out, held[:]).then_inc(out_done, 16)
            pool.wait_ge(out_done, 16)


def edge_pass(nc, a, layer):
    to_src = layer == 2
    gathers = {0: ["src"], 1: ["src", "dst"], 2: ["dst"], 3: ["src"]}[layer]
    to = "src" if to_src else "dst"
    attrs = {0: ["e32"], 1: ["unit", "weight"], 2: [], 3: ["e4"]}[layer]
    width = {"e32": 32, "unit": 3, "weight": 1, "e4": 4}
    emb = {1: EMB1, 3: EMB3}.get(layer)
    LOADS = 16 * (3 + len(attrs) + bool(emb))
    GATHERED = 16 * T * len(gathers)
    SCATTERED = 16 * T
    STEPS = {0: 9, 1: 14, 2: 6, 3: 10}[layer]

    with ExitStack() as ctx:
        sem = Sems(nc, ctx, f"edge{layer}")
        sb = lambda name, shape, dt=F32: ctx.enter_context(nc.sbuf_tensor(f"L{layer}_{name}", shape, dt))
        ps = lambda name, shape, dt=F32: ctx.enter_context(nc.psum_tensor(f"L{layer}_{name}", shape, dt))
        idx = {n: [sb(f"i_{n}{s}", [P, T], I32) for s in range(UNROLL)] for n in ("src", "dst")}
        row = [sb(f"row{s}", [P, T, P], I32) for s in range(UNROLL)]
        attr = {n: [sb(f"a_{n}{s}", [P, T, width[n]]) for s in range(UNROLL)] for n in attrs}
        embt = [sb(f"embt{s}", [emb, GE]) for s in range(UNROLL)] if emb else None
        got = {n: [sb(f"g_{n}{s}", [P, T, D]) for s in range(2)] for n in gathers}
        msg = [sb(f"msg{s}", [P, T, D]) for s in range(2)] if layer != 2 else got["dst"]
        summed = [sb(f"summed{s}", [P, T, D]) for s in range(2)]
        slot_idx = [sb(f"slot_idx{s}", [P, T], I32) for s in range(2)]
        same = [sb(f"same{s}", [P, T, P]) for s in range(2)]
        earlier = sb("earlier", [P, T, P])
        idxf = sb("idxf", [P, T])
        repeat = sb("repeat", [P, T])
        before = sb("before", [P, P])
        trash = sb("trash", [P, 1])
        p_sum = ps("p_sum", [P, T, D])
        loaded = [sem(f"loaded{s}") for s in range(UNROLL)]
        gathered = [sem(f"gathered{s}") for s in range(2)]
        scattered = [sem(f"scattered{s}") for s in range(2)]
        v, load_used, got_used, same_ready, slot_ready, msg_ready, sum_ready, summed_ready, const, const2, weights_in, weights_ready = (
            sem(n) for n in ("v", "load_used", "got_used", "same_ready", "slot_ready", "msg_ready", "sum_ready", "summed_ready",
                             "const", "const2", "weights_in", "weights_ready"))
        if layer == 0:
            lo_row = sb("lo_row", [P, P])
            bits = sb("bits", [P, 2, T], I32)
            bitf = sb("bitf", [P, 2, T])
            hot_lo = [sb(f"hot_lo{s}", [P, T, P], BF16) for s in range(2)]
            hot_hi = [sb(f"hot_hi{s}", [P, T, HI], BF16) for s in range(2)]
            p_deg = ps("p_deg", [HI, P])
            deg_sb = sb("deg_sb", [HI, P])
            no_hot = sb("no_hot", [P, P], BF16)
            zero_ready = sem("zero_ready")
            deg_ready, deg_copied, deg_out = sem("deg_ready"), sem("deg_copied"), sem("deg_out")
        if layer == 1:
            w1 = sb("w1", [EMB1, HID1])
            w2_in = sb("w2_in", [HID1, 7, MUL1, OUT1])
            w2 = sb("w2", [HID1, 1024])
            vec_w = sb("vec_w", [HID1, MUL1, OUT1])
            vec_w_ready = sem("vec_w_ready")
            ht = [sb(f"ht{s}", [HID1, GE]) for s in range(2)]
            u32 = sb("u32", [P, T, 32])
            v16 = sb("v16", [P, T, MUL1, 3])
            dots = sb("dots", [P, T, MUL1, 3])
            prod = sb("prod", [P, T, 24 * 32])
            prodv = sb("prodv", [P, T, 24 * 16])
            red = sb("red", [P, T, 24])
            redv = sb("redv", [P, T, 24])
            gate = [sb(f"gate{s}", [P, T, 16]) for s in range(2)]
            vout = sb("vout", [P, T, 8, 3])
            wn = sb("wn", [P, T])
            p_h = ps("p_h", [HID1, 2, 512])
            p_w = [ps(f"p_w{s}", [P, 1024]) for s in range(2)]
        if layer == 3:
            w1 = sb("w1", [EMB3, HID3])
            w2_in = sb("w2_in", [P, 2, 4, MUL3, MUL3])
            w2 = sb("w2", [P, 2, 256])
            ht = [sb(f"ht{s}", [P, 2, GE]) for s in range(2)]
            x16 = sb("x16", [P, T, 16])
            sv = sb("sv", [P, T, 3, MUL3])
            dots = sb("dots", [P, T, MUL3, 3])
            prods = sb("prods", [P, T, 128])
            prodt = sb("prodt", [P, T, 64])
            prodv = sb("prodv", [P, T * 3, 64])
            rt = sb("rt", [P, T, 8])
            rv = sb("rv", [P, T * 3, 8])
            vout = sb("vout", [P, T, 8, 3])
            p_h = ps("p_h", [P, 4, 512])
            p_w = ps("p_w", [P, 3 * 512])
        if emb:
            h_mm, ht_ready, w_mm, w_used, red_ready, gate_ready = (
                sem(n) for n in ("h_mm", "ht_ready", "w_mm", "w_used", "red_ready", "gate_ready"))
        block = ctx.enter_context(nc.Block())
        h_per = {1: 1, 3: 1}.get(layer)

        @block.sync
        def _(sp):
            if emb:
                sp.dma_start(w1[:], a[f"w1_{layer}"]).then_inc(weights_in, 16)
                sp.dma_start(w2_in[:], a[f"w2_{layer}"]).then_inc(weights_in, 16)

            def load(g):
                s, s2 = g.slot(UNROLL), g.slot(2)
                wait_count(sp, load_used, g.times(1, 1 - UNROLL))
                if emb:
                    wait_count(sp, h_mm, g.times(1, 1 - UNROLL))
                wait_count(sp, gathered[s2], g.turn(2) * GATHERED - GATHERED * (UNROLL // 2 - 1))
                at = g.times(1)
                for n in ("src", "dst"):
                    sp.dma_start(idx[n][s][:], pick(a[n], at)).then_inc(loaded[s], 16)
                sp.dma_start(row[s][:].rearrange("p t q -> p (t q)"),
                             a[f"{to}_row"][bass.ds(at, 1), :].to_broadcast([P, GE])).then_inc(loaded[s], 16)
                for n in attrs:
                    sp.dma_start(attr[n][s][:].rearrange("p t c -> p (t c)"), pick(a[n], at)).then_inc(loaded[s], 16)
                if emb:
                    sp.dma_start(embt[s][:], pick(a[f"emb{layer}"], at)).then_inc(loaded[s], 16)

            groups(sp, load)
            if layer == 0:
                sp.wait_ge(deg_copied, 1)
                sp.dma_start(a["deg"].rearrange("(h l) o -> h (l o)", l=P), deg_sb[:]).then_inc(deg_out, 16)
                sp.wait_ge(deg_out, 16)

        @block.gpsimd
        def _(pool):
            pool.memset(before[:], 1.0).then_inc(const, 1)
            pool.iota(trash[:], [[0, 1]], base=N, channel_multiplier=1, allow_small_or_imprecise_dtypes=True)
            if layer == 0:
                pool.memset(no_hot[:], 0.0).then_inc(zero_ready, 1)
                pool.iota(lo_row[:], [[1, P]], base=0, channel_multiplier=0, allow_small_or_imprecise_dtypes=True)
            pool.wait_ge(const, 1)
            pool.affine_select(out=before[:], in_=before[:], compare_op=ALU.is_gt, fill=0.0, base=0,
                               pattern=[[-1, P]], channel_multiplier=1).then_inc(const2, 1)

            def gather(g):
                s, s2 = g.slot(UNROLL), g.slot(2)
                wait_count(pool, sum_ready if layer == 2 else got_used, g.times(1, -1))
                pool.nop(nofuse=True)
                wait_count(pool, loaded[s], g.turn(UNROLL) * LOADS + LOADS)
                pool.nop(nofuse=True)
                for n in gathers:
                    for t in range(T):
                        pool.indirect_dma_start(
                            out=got[n][s2][:, t, :], out_offset=None, in_=a["table"][layer + 0].rearrange("p (j d) -> (p j) d", d=D),
                            in_offset=bass.IndirectOffsetOnAxis(ap=idx[n][s][:, t:t + 1], axis=0),
                        ).then_inc(gathered[s2], 16)

            def scatter(g):
                s2 = g.slot(2)
                pool.wait_ge(slot_ready, g.times(1, 1))
                pool.nop(nofuse=True)
                pool.wait_ge(summed_ready, g.times(1, 1))
                pool.nop(nofuse=True)
                wait_count(pool, scattered[1 - s2], (g.turn(2) + s2) * SCATTERED)
                pool.nop(nofuse=True)
                for t in range(T):
                    pool.indirect_dma_start(
                        out=a["acc"][layer][t], out_offset=bass.IndirectOffsetOnAxis(ap=slot_idx[s2][:, t:t + 1], axis=0),
                        in_=summed[s2][:, t, :], in_offset=None, compute_op=ALU.add,
                    ).then_inc(scattered[s2], 16)

            def step(g):
                gather(g)
                if g.base >= 2:
                    scatter(Group(g.base - 2, g.i))

            groups(pool, step)
            for g in (G - 2, G - 1):
                scatter(Group(g))
            for s in range(2):
                pool.wait_ge(scattered[s], SCATTERED * ((G + 1 - s) // 2))

        @block.vector
        def _(dve):
            vec = nc.vector
            if layer == 1:
                dve.wait_ge(weights_in, 32)
                w4 = w2[:, 0:768].rearrange("h (o u) -> h o u", u=32)
                r = [w2_in[:, i, :, :].rearrange("h u w -> h w u") for i in range(7)]
                vec.tensor_copy(w4[:, 0:8, 0:16], r[0])
                vec.tensor_copy(w4[:, 0:8, 16:32], r[1])
                vec.tensor_copy(w4[:, 8:16, 0:16], r[2])
                vec.tensor_copy(w4[:, 8:16, 16:32], r[3])
                vec.tensor_copy(w4[:, 16:24, 0:16], r[4])
                vec.tensor_scalar_mul(w4[:, 16:24, 16:32], r[6], 1.5 ** 0.5)
                vec.tensor_scalar_mul(vec_w[:], w2_in[:, 6, :, :], -(1.5 ** 0.5) / 3.0).then_inc(vec_w_ready, 1)
                dve.wait_ge(vec_w_ready, 1)
                vec.scalar_tensor_tensor(w2[:, 768:896].rearrange("h (w u) -> h w u", u=16), r[5], 3.0 ** -0.5,
                                         vec_w[:].rearrange("h u w -> h w u"), ALU.mult, ALU.add
                                         ).then_inc(weights_ready, 1)
            if layer == 3:
                dve.wait_ge(weights_in, 32)
                for k in range(2):
                    r = [w2_in[:, k, i, :, :].rearrange("h u w -> h w u") for i in range(4)]
                    w4 = w2[:, k, 0:128].rearrange("h (o u) -> h o u", u=16)
                    vec.tensor_copy(w4[:, :, 0:8], r[0])
                    vec.tensor_scalar_mul(w4[:, :, 8:16], r[1], 3.0 ** -0.5)
                    vec.tensor_copy(w2[:, k, 128:192].rearrange("h (o u) -> h o u", u=8), r[2])
                    last = vec.tensor_copy(w2[:, k, 192:256].rearrange("h (o u) -> h o u", u=8), r[3])
                last.then_inc(weights_ready, 1)
            dve.wait_ge(const2, 1)

            def body(g):
                s, s2 = g.slot(UNROLL), g.slot(2)
                done = [0]

                def link(ins):
                    done[0] += 1
                    ins.then_inc(v, 1)
                    dve.wait_ge(v, g.times(STEPS, done[0]))

                dve.wait_ge(loaded[s], g.turn(UNROLL) * LOADS + LOADS)
                link(vec.tensor_copy(idxf[:], idx[to][s][:]))
                wait_count(dve, sum_ready, g.times(1, -1))
                vec.tensor_tensor(same[s2][:], row[s][:], spread(idxf[:], [P, T, P], 2), ALU.is_equal
                                  ).then_inc(same_ready, 1)
                dve.wait_ge(same_ready, g.times(1, 1))
                link(vec.tensor_mul(earlier[:], same[s2][:], spread(before[:], [P, T, P], 1)))
                link(vec.tensor_reduce(repeat[:], earlier[:], AX.X, ALU.add))
                link(vec.tensor_scalar_min(repeat[:], repeat[:], 1.0))
                link(vec.tensor_scalar(earlier[:, :, 0], idxf[:], -1.0, trash[:, 0:1], ALU.mult, ALU.add))
                link(vec.tensor_mul(repeat[:], repeat[:], earlier[:, :, 0]))
                wait_count(dve, scattered[s2], g.turn(2) * SCATTERED)
                vec.tensor_add(slot_idx[s2][:], idxf[:], repeat[:]).then_inc(slot_ready, 1)
                dve.wait_ge(slot_ready, g.times(1, 1))
                if layer == 0:
                    vec.tensor_single_scalar(bits[:, 0, :], idx["src"][s][:], P - 1, ALU.bitwise_and)
                    link(vec.tensor_single_scalar(bits[:, 1, :], idx["src"][s][:], 7, ALU.logical_shift_right))
                    link(vec.tensor_copy(bitf[:], bits[:]))
                    vec.tensor_tensor(hot_lo[s2][:], spread(lo_row[:], [P, T, P], 1), spread(bitf[:, 0, :], [P, T, P], 2), ALU.is_equal)
                    vec.tensor_tensor(hot_hi[s2][:], spread(lo_row[:, 0:HI], [P, T, HI], 1), spread(bitf[:, 1, :], [P, T, HI], 2), ALU.is_equal)
                dve.wait_ge(gathered[s2], g.turn(2) * GATHERED + GATHERED)
                if layer == 0:
                    link(vec.tensor_add(got["src"][s2][:], got["src"][s2][:], attr["e32"][s][:]))
                    vec.tensor_scalar_max(msg[s2][:], got["src"][s2][:], 0.0).then_inc(msg_ready, 1)
                    dve.wait_ge(msg_ready, g.times(1, 1))
                    vec.sem_inc(got_used)
                    vec.sem_inc(load_used)
                if layer == 2:
                    vec.sem_inc(load_used)
                if layer == 1:
                    gs, gd, n3, wt = got["src"][s2], got["dst"][s2], attr["unit"][s], attr["weight"][s]
                    vec.tensor_copy(u32[:, :, 0:8], gs[:, :, 0:8])
                    vec.tensor_copy(u32[:, :, 8:16], gd[:, :, 0:8])
                    vec.tensor_copy(v16[:, :, 0:8, :].rearrange("p t u c -> p t (u c)"), gs[:, :, 8:32])
                    link(vec.tensor_copy(v16[:, :, 8:16, :].rearrange("p t u c -> p t (u c)"), gd[:, :, 8:32]))
                    link(vec.tensor_mul(dots[:], v16[:], spread(n3[:], [P, T, MUL1, 3], 2)))
                    link(vec.tensor_reduce(u32[:, :, 16:32], dots[:], AX.X, ALU.add))
                    for t in range(T):
                        b = (g.base * T + t) % 2
                        dve.wait_ge(w_mm, g.times(T, t + 1))
                        vec.tensor_mul(prod[:, t, :].rearrange("p (o u) -> p o u", u=32), p_w[b][:, 0:768].rearrange("p (o u) -> p o u", u=32),
                                       spread(u32[:, t, :], [P, 24, 32], 1))
                        vec.tensor_tensor(prodv[:, t, :].rearrange("p (k w u) -> p k w u", w=8, u=16),
                                          spread(p_w[b][:, 768:896].rearrange("p (w u) -> p w u", u=16), [P, 3, 8, 16], 1),
                                          spread(v16[:, t, :, :].rearrange("p u k -> p k u"), [P, 3, 8, 16], 2), ALU.mult
                                          ).then_inc(w_used, 1)
                    dve.wait_ge(w_used, g.times(T, T))
                    vec.tensor_reduce(red[:], prod[:].rearrange("p t (o u) -> p t o u", u=32), AX.X, ALU.add).then_inc(red_ready, 1)
                    vec.tensor_scalar_mul(wn[:], wt[:, :, 0], TANH_GAIN)
                    link(vec.tensor_reduce(redv[:], prodv[:].rearrange("p t (o u) -> p t o u", u=16), AX.X, ALU.add))
                    for t in range(T):
                        ins = vec.tensor_mul(vout[:, t, :, :], spread(red[:, t, 16:24], [P, 8, 3], 2), spread(n3[:, t, :], [P, 8, 3], 1))
                    link(ins)
                    link(vec.tensor_add(vout[:], vout[:], redv[:].rearrange("p t (k w) -> p t w k", w=8)))
                    dve.wait_ge(gate_ready, g.times(1, 1))
                    link(vec.tensor_mul(gate[s2][:], gate[s2][:], spread(wn[:], [P, T, 16], 2)))
                    link(vec.tensor_mul(vout[:], vout[:], spread(gate[s2][:, :, 8:16], [P, T, 8, 3], 3)))
                    vec.tensor_copy(msg[s2][:, :, 0:8], gate[s2][:, :, 0:8])
                    vec.tensor_scalar_mul(msg[s2][:, :, 8:32], vout[:].rearrange("p t w k -> p t (w k)"), 0.25).then_inc(msg_ready, 1)
                    dve.wait_ge(msg_ready, g.times(1, 1))
                    vec.sem_inc(got_used)
                    vec.sem_inc(load_used)
                if layer == 3:
                    gs, sh = got["src"][s2], attr["e4"][s]
                    v8 = gs[:, :, 8:32].rearrange("p t (u k) -> p t u k", k=3)
                    vec.tensor_mul(x16[:, :, 0:8], gs[:, :, 0:8], sh[:, :, 0:1].to_broadcast([P, T, 8]))
                    vec.tensor_mul(sv[:].rearrange("p t k u -> p t u k"), v8, sh[:, :, 0:1].unsqueeze(3).to_broadcast([P, T, 8, 3]))
                    link(vec.tensor_mul(dots[:], v8, spread(sh[:, :, 1:4], [P, T, 8, 3], 2)))
                    link(vec.tensor_reduce(x16[:, :, 8:16], dots[:], AX.X, ALU.add))
                    dve.wait_ge(w_mm, g.times(1, 1))
                    pw = p_w[:, 0:1280].rearrange("p (t c) -> p t c", c=256)
                    vec.tensor_mul(prods[:].rearrange("p t (w u) -> p t w u", u=16), pw[:, :, 0:128].rearrange("p t (w u) -> p t w u", u=16),
                                   spread(x16[:], [P, T, 8, 16], 2))
                    vec.tensor_mul(prodt[:].rearrange("p t (w u) -> p t w u", u=8), pw[:, :, 128:192].rearrange("p t (w u) -> p t w u", u=8),
                                   spread(gs[:, :, 0:8], [P, T, 8, 8], 2))
                    for t in range(T):
                        ins = vec.tensor_tensor(prodv[:, 3 * t:3 * t + 3, :].rearrange("p k (w u) -> p k w u", u=8),
                                                spread(pw[:, t, 192:256].rearrange("p (w u) -> p w u", u=8), [P, 3, 8, 8], 1),
                                                spread(sv[:, t, :, :], [P, 3, 8, 8], 2), ALU.mult)
                    ins.then_inc(w_used, 1)
                    dve.wait_ge(w_used, g.times(1, 1))
                    vec.tensor_reduce(msg[s2][:, :, 0:8], prods[:].rearrange("p t (w u) -> p t w u", u=16), AX.X, ALU.add)
                    vec.tensor_reduce(rt[:], prodt[:].rearrange("p t (w u) -> p t w u", u=8), AX.X, ALU.add)
                    link(vec.tensor_reduce(rv[:], prodv[:].rearrange("p t (w u) -> p t w u", u=8), AX.X, ALU.add))
                    for t in range(T):
                        ins = vec.tensor_mul(vout[:, t, :, :], spread(rt[:, t, :], [P, 8, 3], 2), spread(sh[:, t, 1:4], [P, 8, 3], 1))
                    link(ins)
                    vec.tensor_add(msg[s2][:, :, 8:32].rearrange("p t (w k) -> p t w k", k=3), vout[:],
                                   rv[:].rearrange("p (t k) w -> p t w k", k=3)).then_inc(msg_ready, 1)
                    dve.wait_ge(msg_ready, g.times(1, 1))
                    vec.sem_inc(got_used)
                    vec.sem_inc(load_used)
                assert done[0] == STEPS, (layer, done[0])

            groups(dve, body)
            if layer == 0:
                dve.wait_ge(deg_ready, 1)
                vec.tensor_copy(deg_sb[:], p_deg[:]).then_inc(deg_copied, 1)

        @block.tensor
        def _(pe):
            def sum_repeats(g):
                s2 = g.slot(2)
                pe.wait_ge(same_ready, g.times(1, 1))
                if layer == 2:
                    pe.wait_ge(gathered[s2], g.turn(2) * GATHERED + GATHERED)
                else:
                    pe.wait_ge(msg_ready, g.times(1, 1))
                wait_count(pe, summed_ready, g.times(1))
                if layer == 0:
                    for t in range(T):
                        nc.tensor.matmul(p_deg[:], hot_hi[s2][:, t, :], hot_lo[s2][:, t, :],
                                         start=False, stop=False, skip_group_check=True)
                for t in range(T):
                    last = nc.tensor.matmul(p_sum[:, t, :], same[s2][:, t, :], msg[s2][:, t, :], start=True, stop=True)
                last.then_inc(sum_ready, 1)

            def body(g):
                s, s2 = g.slot(UNROLL), g.slot(2)
                if layer == 1:
                    pe.wait_ge(loaded[s], g.turn(UNROLL) * LOADS + LOADS)
                    wait_count(pe, ht_ready, g.times(1))
                    pe.nop(nofuse=True)
                    for c in range(2):
                        last = nc.tensor.matmul(p_h[:, c, 0:GE // 2], w1[:], embt[s][:, c * (GE // 2):(c + 1) * (GE // 2)],
                                                start=True, stop=True)
                    last.then_inc(h_mm, 1)
                    pe.wait_ge(ht_ready, g.times(1, 1))
                    for t in range(T):
                        if t == 2 and g.base >= 1:
                            sum_repeats(Group(g.base - 1, g.i))
                        b = (g.base * T + t) % 2
                        wait_count(pe, w_used, g.times(T, t - 1))
                        for c0, c1 in ((0, 512), (512, 896)):
                            last = nc.tensor.matmul(p_w[b][:, c0:c1], ht[s2][:, t * P:(t + 1) * P], w2[:, c0:c1],
                                                    start=True, stop=True)
                        last.then_inc(w_mm, 1)
                elif layer == 3:
                    pe.wait_ge(loaded[s], g.turn(UNROLL) * LOADS + LOADS)
                    wait_count(pe, ht_ready, g.times(1))
                    pe.nop(nofuse=True)
                    for k in range(2):
                        for c in range(2):
                            last = nc.tensor.matmul(p_h[:, 2 * k + c, 0:GE // 2], w1[:, k * P:(k + 1) * P],
                                                    embt[s][:, c * (GE // 2):(c + 1) * (GE // 2)], start=True, stop=True)
                    last.then_inc(h_mm, 1)
                    if g.base >= 1:
                        sum_repeats(Group(g.base - 1, g.i))
                    pe.wait_ge(ht_ready, g.times(1, 1))
                    wait_count(pe, w_used, g.times(1))
                    for t in range(T):
                        for k in range(2):
                            last = nc.tensor.matmul(p_w[:, t * 256:(t + 1) * 256], ht[s2][:, k, t * P:(t + 1) * P], w2[:, k, :],
                                                    start=k == 0, stop=k == 1)
                    last.then_inc(w_mm, 1)
                else:
                    sum_repeats(g)

            if emb:
                pe.wait_ge(weights_ready, 1)
            if layer == 0:
                pe.wait_ge(zero_ready, 1)
                nc.tensor.matmul(p_deg[:], no_hot[:, 0:HI], no_hot[:], start=True, stop=False, skip_group_check=True)
            groups(pe, body)
            if emb:
                sum_repeats(Group(G - 1))
            if layer == 0:
                nc.tensor.matmul(p_deg[:], no_hot[:, 0:HI], no_hot[:], start=False, stop=True, skip_group_check=True
                                 ).then_inc(deg_ready, 1)

        @block.scalar
        def _(act):
            def copy_sums(g):
                s2 = g.slot(2)
                act.wait_ge(sum_ready, g.times(1, 1))
                wait_count(act, scattered[s2], g.turn(2) * SCATTERED)
                ins = nc.scalar.copy(summed[s2][:], p_sum[:])
                ins.then_inc(summed_ready, 1)

            def body(g):
                s2 = g.slot(2)
                if layer == 1:
                    act.wait_ge(h_mm, g.times(1, 1))
                    wait_count(act, w_mm, g.times(T, -T))
                    nc.scalar.activation(ht[s2][:].rearrange("h (c e) -> h c e", c=2), p_h[:, :, 0:GE // 2], ACT.Relu,
                                         scale=0.2 ** 0.5 / 4.0).then_inc(ht_ready, 1)
                    if g.base >= 1:
                        copy_sums(Group(g.base - 1, g.i))
                    act.wait_ge(red_ready, g.times(1, 1))
                    wait_count(act, msg_ready, g.times(1, -1))
                    nc.scalar.activation(gate[s2][:], red[:, :, 0:16], ACT.Tanh, scale=1.0 / 32 ** 0.5).then_inc(gate_ready, 1)
                elif layer == 3:
                    act.wait_ge(h_mm, g.times(1, 1))
                    wait_count(act, w_mm, g.times(1, -1))
                    nc.scalar.activation(ht[s2][:].rearrange("h k (c e) -> h (k c) e", c=2), p_h[:, :, 0:GE // 2], ACT.Relu,
                                         scale=0.5 / 16.0 * (1.0 / 128.0) ** 0.5 / (E / N) ** 0.5).then_inc(ht_ready, 1)
                    if g.base >= 1:
                        copy_sums(Group(g.base - 1, g.i))
                else:
                    copy_sums(g)

            groups(act, body)
            if emb:
                copy_sums(Group(G - 1))


def pick(table, at):
    return table[bass.ds(at, 1), :, :].rearrange("g p c -> (g p) c")


def build(nc, x, src, dst, src_row, dst_row, emb10, vec3, e32, e4, emb8, weight, eps, w1_1, w2_1, w1_3, w2_3, out):
    def dram(name, shape, dt=F32):
        return nc.dram_tensor(name, shape, dt, kind="Internal").ap()

    a = {
        "x": x, "src": src, "dst": dst, "src_row": src_row, "dst_row": dst_row, "e32": e32, "e4": e4,
        "weight": weight, "eps": eps, "emb1": emb10, "emb3": emb8, "out": out,
        "w1_1": w1_1, "w2_1": w2_1, "w1_3": w1_3, "w2_3": w2_3, "unit_in": vec3,
        "table": [dram(f"table{i}", (NP, NJ * D)) for i in range(4)],
        "acc": [[dram(f"acc{i}_{t}", (N + TRASH, D)) for t in range(T)] for i in range(4)],
        "deg": dram("deg", (HI * P, 1)),
    }
    unit = dram("unit", (E, 3))
    a["unit"] = unit.rearrange("(p e) c -> p (e c)", p=NP)
    with ExitStack() as ctx:
        a["x_sb"] = ctx.enter_context(nc.sbuf_tensor("x_sb", [NP, NJ * D], F32))
        a["h_sb"] = ctx.enter_context(nc.sbuf_tensor("h_sb", [NP, NJ * D], F32))
        a["norm_sb"] = ctx.enter_context(nc.sbuf_tensor("norm_sb", [NP, NJ], F32))
        setup_pass(nc, a)
        a["unit"] = unit.rearrange("(g p t) c -> g p (t c)", p=P, t=T)
        for layer in range(4):
            node_pass(nc, a, layer)
            edge_pass(nc, a, layer)
        node_pass(nc, a, 4)


def kernel(x, src, dst, edge_attr_10, edge_attr_3, edge_attr_32, edge_attr_4, edge_attr_8, edge_weight,
           L0_gnn_eps, L1_gnn_W1, L1_gnn_W2, L3_gnn_fc_w1, L3_gnn_fc_w2):
    import numpy as np
    import concourse.bacc as bacc
    from concourse.bass_utils import run_bass_kernel_spmd

    c = np.ascontiguousarray

    def columns(z):
        return c(np.asarray(z).reshape(G, P, T, -1).transpose(0, 3, 2, 1).reshape(G, -1, GE))

    arrays = {
        "x": c(np.asarray(x).reshape(NP, NJ * D)),
        "src": c(np.asarray(src).reshape(G, P, T)),
        "dst": c(np.asarray(dst).reshape(G, P, T)),
        "src_row": columns(src).reshape(G, GE),
        "dst_row": columns(dst).reshape(G, GE),
        "emb10": columns(edge_attr_10),
        "vec3": c(np.asarray(edge_attr_3).reshape(NP, EJ * 3)),
        "e32": c(np.asarray(edge_attr_32).reshape(G, P, T * 32)),
        "e4": c(np.asarray(edge_attr_4).reshape(G, P, T * 4)),
        "emb8": columns(edge_attr_8),
        "weight": c(np.asarray(edge_weight).reshape(G, P, T)),
        "eps": c(np.broadcast_to(np.asarray(L0_gnn_eps).reshape(1, 1), (NP, 1))),
        "w1_1": c(np.asarray(L1_gnn_W1)),
        "w2_1": c(np.asarray(L1_gnn_W2).reshape(HID1, 7, MUL1, OUT1)),
        "w1_3": c(np.asarray(L3_gnn_fc_w1)),
        "w2_3": c(np.asarray(L3_gnn_fc_w2).reshape(2, P, 4, MUL3, MUL3).transpose(1, 0, 2, 3, 4)),
    }
    nc = bacc.Bacc("TRN2", target_bir_lowering=False, num_devices=1)
    args = [nc.dram_tensor(name, z.shape, mybir.dt.from_np(z.dtype), kind="ExternalInput").ap() for name, z in arrays.items()]
    out = nc.dram_tensor("out", (NP, NJ * D), F32, kind="ExternalOutput").ap()
    build(nc, *args, out)
    r = run_bass_kernel_spmd(nc, [arrays], core_ids=[0])
    return r.results[0]["out"].reshape(N, D)
```

```python
from contextlib import ExitStack

import concourse.bass as bass
from concourse import mybir

F32 = mybir.dt.float32
BF16 = mybir.dt.bfloat16
I32 = mybir.dt.int32
ALU = mybir.AluOpType
ACT = mybir.ActivationFunctionType
AX = mybir.AxisListType

N, D, E = 12500, 32, 400000
P = 128
T = 5
GE = P * T
G = E // GE
NP, NJ = 125, N // 125
EJ = E // NP
UNROLL = 4
PEEL = G - (G - 2 * UNROLL + 3) // UNROLL * UNROLL
TRASH = P
WIN = P
HI = (N + P - 1) // P
MUL1, OUT1, HID1, EMB1 = 16, 8, 16, 10
MUL3, HID3, EMB3 = 8, 256, 8
EPS = 1e-5
TANH_GAIN = 1.593


class Group:

    def __init__(self, base, i=None):
        self.base, self.i = base, i

    def slot(self, n):
        return self.base % n

    def times(self, per, more=0):
        at = per * self.base + more
        return at if self.i is None else self.i * (per * UNROLL) + at

    def turn(self, n):
        at = self.base // n
        return at if self.i is None else self.i * (UNROLL // n) + at


def wait_count(eng, sem, count):
    if isinstance(count, int) and count <= 0:
        return
    eng.wait_ge(sem, count)


def groups(eng, body):
    for g in range(PEEL):
        body(Group(g))
    with eng.Fori(0, (G - PEEL) // UNROLL) as i:
        for c in range(UNROLL):
            body(Group(PEEL + c, i))


assert PEEL >= UNROLL + 1 and (G - PEEL) % UNROLL == 0


def spread(ap, shape, axis):
    return ap.unsqueeze(axis).to_broadcast(shape)


class Sems:

    def __init__(self, nc, prefix):
        self.nc, self.prefix, self.made = nc, prefix, {}

    def __call__(self, name):
        if name not in self.made:
            self.made[name] = self.nc.alloc_semaphore(f"{self.prefix}_{name}")
        return self.made[name]

    def clear(self):
        self.nc.clear_and_free_semaphores(list(self.made.values()))
        self.nc.all_engine_barrier()


def setup_pass(nc, a):
    with ExitStack() as ctx:
        sem = Sems(nc, "setup")
        sb = lambda name, shape, dt=F32: ctx.enter_context(nc.sbuf_tensor(name, shape, dt))
        zeros = sb("zeros", [P, NJ * D])
        vec = sb("vec", [NP, EJ * 3])
        square = sb("square", [NP, EJ * 3])
        length = sb("length", [NP, EJ])
        zeroed, x_in, vec_in, lengths, roots, v_step, unit_out, zero_out = (
            sem(n) for n in ("zeroed", "x_in", "vec_in", "lengths", "roots", "v_step", "unit_out", "zero_out"))
        consts = sem("consts")
        block = ctx.enter_context(nc.Block())

        @block.gpsimd
        def _(pool):
            pool.memset(zeros[:], 0.0).then_inc(zeroed, 1)
            pool.iota(a["row_iota"][:], [[1, P]], base=0, channel_multiplier=0, allow_small_or_imprecise_dtypes=True)
            pool.iota(a["col_iota"][:], [[0, 1]], base=0, channel_multiplier=1, allow_small_or_imprecise_dtypes=True)
            pool.iota(a["trash"][:], [[0, 1]], base=N, channel_multiplier=1, allow_small_or_imprecise_dtypes=True)
            pool.memset(a["before"][:], 1.0).then_inc(consts, 1)
            pool.memset(a["ident"][:], 0.0).then_inc(consts, 1)
            pool.wait_ge(consts, 2)
            pool.affine_select(out=a["before"][:], in_=a["before"][:], compare_op=ALU.is_gt, fill=0.0, base=0,
                               pattern=[[-1, P]], channel_multiplier=1).then_inc(consts, 1)
            pool.affine_select(out=a["ident"][:], in_=a["ident"][:], compare_op=ALU.not_equal, fill=1.0, base=0,
                               pattern=[[-1, P]], channel_multiplier=1).then_inc(consts, 1)
            pool.wait_ge(consts, 4)

        @block.sync
        def _(sp):
            sp.dma_start(vec[:], a["unit_in"]).then_inc(vec_in, 16)
            sp.dma_start(a["x_sb"][:], a["x"]).then_inc(x_in, 16)
            sp.wait_ge(zeroed, 1)
            n = 32 * T
            for rows in a["acc"][2]:
                flat = rows[0:N, :].rearrange("(p r) d -> p (r d)", p=NP)
                sp.dma_start(flat, zeros[0:NP, :]).then_inc(zero_out, 16)
                sp.dma_start(rows[N:N + TRASH, :], zeros[0:TRASH, 0:D]).then_inc(zero_out, 16)
            for table in a["table"]:
                sp.dma_start(table[N:N + WIN, :], zeros[0:WIN, 0:D]).then_inc(zero_out, 16)
                n += 16
            for table in a["split"].values():
                sp.dma_start(table[N:N + WIN, :], zeros[0:WIN, 0:3 * D // 2].bitcast(BF16)).then_inc(zero_out, 16)
                n += 16
            sp.wait_ge(v_step, 4)
            sp.dma_start(a["unit"], vec[:]).then_inc(unit_out, 16)
            sp.wait_ge(zero_out, n)
            sp.wait_ge(unit_out, 16)
            sp.wait_ge(x_in, 16)

        @block.scalar
        def _(act):
            act.wait_ge(lengths, 1)
            nc.scalar.activation(length[:], length[:], ACT.Sqrt).then_inc(roots, 1)

        @block.vector
        def _(dve):
            v3 = vec[:].rearrange("p (e c) -> p e c", c=3)
            s3 = square[:].rearrange("p (e c) -> p e c", c=3)
            dve.wait_ge(vec_in, 16)
            nc.vector.tensor_mul(square[:], vec[:], vec[:]).then_inc(v_step, 1)
            dve.wait_ge(v_step, 1)
            nc.vector.tensor_reduce(length[:], s3, AX.X, ALU.add).then_inc(lengths, 1)
            dve.wait_ge(roots, 1)
            nc.vector.reciprocal(length[:], length[:]).then_inc(v_step, 1)
            dve.wait_ge(v_step, 2)
            nc.vector.tensor_mul(v3, v3, spread(length[:], [NP, EJ, 3], 2)).then_inc(v_step, 2)
    sem.clear()


def node_pass(nc, a, layer):
    with ExitStack() as ctx:
        sem = Sems(nc, f"node{layer}")
        sb = lambda name, shape, dt=F32: ctx.enter_context(nc.sbuf_tensor(f"L{layer}_{name}", shape, dt))
        sums = a["sums_sb"]
        work = sb("work", [NP, NJ * D])
        stat = sb("stat", [NP, NJ])
        deg = sb("deg", [NP, NJ]) if layer == 2 else None
        eps = sb("eps", [NP, 1]) if layer == 1 else None
        deg_in, eps_in, v, var_ready, root_ready, deg1_ready, degroot_ready, out_done = (
            sem(n) for n in ("deg_in", "eps_in", "v", "var_ready", "root_ready", "deg1_ready", "degroot_ready", "out_done"))
        acc_zero, split_out = sem("acc_zero"), sem("split_out")
        parts = sb("parts", [NP, NJ * D * 3], BF16) if layer in (1, 2) else None
        x, h, norm = a["x_sb"], a["h_sb"], a["norm_sb"]
        x3, h3, w3 = (z[:].rearrange("p (j d) -> p j d", d=D) for z in (x, h, work))
        block = ctx.enter_context(nc.Block())
        steps = [0]

        @block.sync
        def _(sp):
            if layer == 1:
                sp.dma_start(eps[:], a["eps"]).then_inc(eps_in, 16)
            if layer == 2:
                sp.dma_start(deg[:], a["deg"][0:N, :].rearrange("(p j) o -> p (j o)", p=NP)).then_inc(deg_in, 16)

        @block.scalar
        def _(act):
            if layer == 2:
                act.wait_ge(deg1_ready, 1)
                nc.scalar.activation(norm[:], norm[:], ACT.Sqrt).then_inc(degroot_ready, 1)
            if layer < 4:
                act.wait_ge(var_ready, 1)
                nc.scalar.activation(stat[:], stat[:], ACT.Sqrt).then_inc(root_ready, 1)

        @block.vector
        def _(dve):
            def link(ins):
                steps[0] += 1
                ins.then_inc(v, 1)
                dve.wait_ge(v, steps[0])

            if layer == 1:
                dve.wait_ge(eps_in, 16)
                link(nc.vector.tensor_scalar_add(eps[:], eps[:], 1.0))
                link(nc.vector.scalar_tensor_tensor(work[:], h[:], eps[:, 0:1], sums[:], ALU.mult, ALU.add))
                link(nc.vector.tensor_add(x[:], x[:], work[:]))
            elif layer == 2:
                link(nc.vector.tensor_add(x[:], x[:], sums[:]))
                dve.wait_ge(deg_in, 16)
                nc.vector.tensor_scalar_add(norm[:], deg[:], 1.0).then_inc(deg1_ready, 1)
                dve.wait_ge(degroot_ready, 1)
                link(nc.vector.reciprocal(norm[:], norm[:]))
            elif layer == 3:
                link(nc.vector.tensor_add(work[:], sums[:], h[:]))
                link(nc.vector.tensor_mul(w3, w3, spread(norm[:], [NP, NJ, D], 2)))
                link(nc.vector.tensor_add(x[:], x[:], work[:]))
            elif layer == 4:
                link(nc.vector.tensor_add(x[:], x[:], sums[:]))
            if layer < 4:
                link(nc.vector.tensor_reduce(stat[:], x3, AX.X, ALU.add))
                link(nc.vector.tensor_scalar_mul(stat[:], stat[:], 1.0 / D))
                link(nc.vector.tensor_tensor(h3, x3, spread(stat[:], [NP, NJ, D], 2), ALU.subtract))
                link(nc.vector.tensor_mul(work[:], h[:], h[:]))
                link(nc.vector.tensor_reduce(stat[:], w3, AX.X, ALU.add))
                nc.vector.tensor_scalar(stat[:], stat[:], 1.0 / D, EPS, ALU.mult, ALU.add).then_inc(var_ready, 1)
                dve.wait_ge(root_ready, 1)
                link(nc.vector.reciprocal(stat[:], stat[:]))
                link(nc.vector.tensor_mul(h3, h3, spread(stat[:], [NP, NJ, D], 2)))
                link(nc.vector.tensor_scalar_max(h[:], h[:], 0.0))
                if layer == 2:
                    link(nc.vector.tensor_mul(h3, h3, spread(norm[:], [NP, NJ, D], 2)))
                if layer in (1, 2):
                    p4 = parts[:].rearrange("p (j s d) -> p s j d", s=3, d=D)
                    link(nc.vector.tensor_copy(p4[:, 0], h3))
                    link(nc.vector.tensor_sub(w3, h3, p4[:, 0]))
                    link(nc.vector.tensor_copy(p4[:, 1], w3))
                    link(nc.vector.tensor_sub(p4[:, 2], w3, p4[:, 1]))

        @block.gpsimd
        def _(pool):
            if layer in (1, 2):
                pool.wait_ge(v, steps[0])
                pool.dma_start(a["split"][layer][0:N, :].rearrange("(p j) d -> p (j d)", p=NP),
                               parts[:]).then_inc(split_out, 16)
                pool.wait_ge(split_out, 16)
            if layer in (0, 1, 3):
                pool.memset(a["acc_t"][:], 0.0).then_inc(acc_zero, 1)
            pool.wait_ge(v, steps[0])
            if layer < 4:
                out, held = a["table"][layer][0:N, :].rearrange("(p j) d -> p (j d)", p=NP), h
            else:
                out, held = a["out"], x
            pool.dma_start(out, held[:]).then_inc(out_done, 16)
            pool.wait_ge(out_done, 16)
    sem.clear()


def edge_pass(nc, a, layer):
    to_src = layer == 2
    gathers = {0: ["src"], 1: ["src", "dst"], 2: ["dst"], 3: ["src"]}[layer]
    to = "src" if to_src else "dst"
    attrs = {0: ["e32"], 1: ["unit", "weight"], 2: [], 3: ["e4"]}[layer]
    width = {"e32": 32, "unit": 3, "weight": 1, "e4": 4}
    emb = {1: EMB1, 3: EMB3}.get(layer)
    LOADS = 16 * (3 + len(attrs) + bool(emb))
    GATHERED = 16 * T * len(gathers)
    SCATTERED = 16 * T
    STEPS = {0: 9, 1: 14, 2: 6, 3: 10}[layer]

    with ExitStack() as ctx:
        sem = a["sems"][layer]
        sb = lambda name, shape, dt=F32: ctx.enter_context(nc.sbuf_tensor(f"g{layer}_{name}", shape, dt))
        ps = lambda name, shape, dt=F32: ctx.enter_context(nc.psum_tensor(f"g{layer}_{name}", shape, dt))
        idx = {n: [sb(f"i_{n}{s}", [P, T], I32) for s in range(UNROLL)] for n in ("src", "dst")}
        row = [sb(f"row{s}", [P, T, P], I32) for s in range(UNROLL)]
        attr = {n: [sb(f"a_{n}{s}", [P, T, width[n]]) for s in range(UNROLL)] for n in attrs}
        embt = [sb(f"embt{s}", [emb, GE]) for s in range(UNROLL)] if emb else None
        got = {n: [sb(f"g_{n}{s}", [P, T, D]) for s in range(2)] for n in gathers}
        msg = [sb(f"msg{s}", [P, T, D]) for s in range(2)] if layer != 2 else got["dst"]
        summed = [sb(f"summed{s}", [P, T, D]) for s in range(2)]
        slot_idx = [sb(f"slot_idx{s}", [P, T], I32) for s in range(2)]
        same = [sb(f"same{s}", [P, T, P]) for s in range(2)]
        earlier = sb("earlier", [P, T, P])
        idxf = sb("idxf", [P, T])
        repeat = sb("repeat", [P, T])
        before = sb("before", [P, P])
        trash = sb("trash", [P, 1])
        p_sum = ps("p_sum", [P, T, D])
        loaded = [sem(f"loaded{s}") for s in range(UNROLL)]
        gathered = [sem(f"gathered{s}") for s in range(2)]
        scattered = [sem(f"scattered{s}") for s in range(2)]
        v, load_used, got_used, same_ready, slot_ready, msg_ready, sum_ready, summed_ready, const, const2, weights_in, weights_ready = (
            sem(n) for n in ("v", "load_used", "got_used", "same_ready", "slot_ready", "msg_ready", "sum_ready", "summed_ready",
                             "const", "const2", "weights_in", "weights_ready"))
        if layer == 0:
            lo_row = sb("lo_row", [P, P])
            bits = sb("bits", [P, 2, T], I32)
            bitf = sb("bitf", [P, 2, T])
            hot_lo = [sb(f"hot_lo{s}", [P, T, P], BF16) for s in range(2)]
            hot_hi = [sb(f"hot_hi{s}", [P, T, HI], BF16) for s in range(2)]
            p_deg = ps("p_deg", [HI, P])
            deg_sb = sb("deg_sb", [HI, P])
            no_hot = sb("no_hot", [P, P], BF16)
            zero_ready = sem("zero_ready")
            deg_ready, deg_copied, deg_out = sem("deg_ready"), sem("deg_copied"), sem("deg_out")
        if layer == 1:
            w1 = sb("w1", [EMB1, HID1])
            w2_in = sb("w2_in", [HID1, 7, MUL1, OUT1])
            w2 = sb("w2", [HID1, 1024])
            vec_w = sb("vec_w", [HID1, MUL1, OUT1])
            vec_w_ready = sem("vec_w_ready")
            ht = [sb(f"ht{s}", [HID1, GE]) for s in range(2)]
            u32 = sb("u32", [P, T, 32])
            v16 = sb("v16", [P, T, MUL1, 3])
            dots = sb("dots", [P, T, MUL1, 3])
            prod = sb("prod", [P, T, 24 * 32])
            prodv = sb("prodv", [P, T, 24 * 16])
            red = sb("red", [P, T, 24])
            redv = sb("redv", [P, T, 24])
            gate = [sb(f"gate{s}", [P, T, 16]) for s in range(2)]
            vout = sb("vout", [P, T, 8, 3])
            wn = sb("wn", [P, T])
            p_h = ps("p_h", [HID1, 1024])
            p_w = [ps(f"p_w{s}", [P, 1024]) for s in range(2)]
        if layer == 3:
            w1 = sb("w1", [EMB3, HID3])
            w2_in = sb("w2_in", [P, 2, 4, MUL3, MUL3])
            w2 = sb("w2", [P, 2, 256])
            ht = [sb(f"ht{s}", [P, 2, GE]) for s in range(2)]
            x16 = sb("x16", [P, T, 16])
            sv = sb("sv", [P, T, 3, MUL3])
            dots = sb("dots", [P, T, MUL3, 3])
            prods = sb("prods", [P, T, 128])
            prodt = sb("prodt", [P, T, 64])
            prodv = sb("prodv", [P, T * 3, 64])
            rt = sb("rt", [P, T, 8])
            rv = sb("rv", [P, T * 3, 8])
            vout = sb("vout", [P, T, 8, 3])
            p_h = [ps(f"p_h{k}", [P, 1024]) for k in range(2)]
            p_w = ps("p_w", [P, 3 * 512])
        if emb:
            h_mm, ht_ready, w_mm, w_used, red_ready, gate_ready = (
                sem(n) for n in ("h_mm", "ht_ready", "w_mm", "w_used", "red_ready", "gate_ready"))
        block = ctx.enter_context(nc.Block())
        h_per = {1: 1, 3: 1}.get(layer)

        @block.sync
        def _(sp):
            if emb:
                sp.dma_start(w1[:], a[f"w1_{layer}"]).then_inc(weights_in, 16)
                sp.dma_start(w2_in[:], a[f"w2_{layer}"]).then_inc(weights_in, 16)

            def load(g):
                s, s2 = g.slot(UNROLL), g.slot(2)
                wait_count(sp, load_used, g.times(1, 1 - UNROLL))
                if emb:
                    wait_count(sp, h_mm, g.times(1, 1 - UNROLL))
                wait_count(sp, gathered[s2], g.turn(2) * GATHERED - GATHERED * (UNROLL // 2 - 1))
                at = g.times(1)
                for n in ("src", "dst"):
                    sp.dma_start(idx[n][s][:], pick(a[n], at)).then_inc(loaded[s], 16)
                sp.dma_start(row[s][:].rearrange("p t q -> p (t q)"),
                             a[f"{to}_row"][bass.ds(at, 1), :].to_broadcast([P, GE])).then_inc(loaded[s], 16)
                for n in attrs:
                    sp.dma_start(attr[n][s][:].rearrange("p t c -> p (t c)"), pick(a[n], at)).then_inc(loaded[s], 16)
                if emb:
                    sp.dma_start(embt[s][:], pick(a[f"emb{layer}"], at)).then_inc(loaded[s], 16)

            groups(sp, load)
            if layer == 0:
                sp.wait_ge(deg_copied, 1)
                sp.dma_start(a["deg"].rearrange("(h l) o -> h (l o)", l=P), deg_sb[:]).then_inc(deg_out, 16)
                sp.wait_ge(deg_out, 16)

        @block.gpsimd
        def _(pool):
            pool.memset(before[:], 1.0).then_inc(const, 1)
            pool.iota(trash[:], [[0, 1]], base=N, channel_multiplier=1, allow_small_or_imprecise_dtypes=True)
            if layer == 0:
                pool.memset(no_hot[:], 0.0).then_inc(zero_ready, 1)
                pool.iota(lo_row[:], [[1, P]], base=0, channel_multiplier=0, allow_small_or_imprecise_dtypes=True)
            pool.wait_ge(const, 1)
            pool.affine_select(out=before[:], in_=before[:], compare_op=ALU.is_gt, fill=0.0, base=0,
                               pattern=[[-1, P]], channel_multiplier=1).then_inc(const2, 1)

            def gather(g):
                s, s2 = g.slot(UNROLL), g.slot(2)
                wait_count(pool, sum_ready if layer == 2 else got_used, g.times(1, -1))
                pool.nop(nofuse=True)
                wait_count(pool, loaded[s], g.turn(UNROLL) * LOADS + LOADS)
                pool.nop(nofuse=True)
                for n in gathers:
                    for t in range(T):
                        pool.indirect_dma_start(
                            out=got[n][s2][:, t, :], out_offset=None, in_=a["table"][layer][0:N, :],
                            in_offset=bass.IndirectOffsetOnAxis(ap=idx[n][s][:, t:t + 1], axis=0),
                        ).then_inc(gathered[s2], 16)

            def scatter(g):
                s2 = g.slot(2)
                pool.wait_ge(slot_ready, g.times(1, 1))
                pool.nop(nofuse=True)
                pool.wait_ge(summed_ready, g.times(1, 1))
                pool.nop(nofuse=True)
                wait_count(pool, scattered[1 - s2], (g.turn(2) + s2) * SCATTERED)
                pool.nop(nofuse=True)
                for t in range(T):
                    pool.indirect_dma_start(
                        out=a["acc"][layer][t], out_offset=bass.IndirectOffsetOnAxis(ap=slot_idx[s2][:, t:t + 1], axis=0),
                        in_=summed[s2][:, t, :], in_offset=None, compute_op=ALU.add,
                    ).then_inc(scattered[s2], 16)

            def step(g):
                gather(g)
                if g.base >= 2:
                    scatter(Group(g.base - 2, g.i))

            groups(pool, step)
            for g in (G - 2, G - 1):
                scatter(Group(g))
            for s in range(2):
                pool.wait_ge(scattered[s], SCATTERED * ((G + 1 - s) // 2))

        @block.vector
        def _(dve):
            vec = nc.vector
            if layer == 1:
                dve.wait_ge(weights_in, 32)
                w4 = w2[:, 0:768].rearrange("h (o u) -> h o u", u=32)
                r = [w2_in[:, i, :, :].rearrange("h u w -> h w u") for i in range(7)]
                vec.tensor_copy(w4[:, 0:8, 0:16], r[0])
                vec.tensor_copy(w4[:, 0:8, 16:32], r[1])
                vec.tensor_copy(w4[:, 8:16, 0:16], r[2])
                vec.tensor_copy(w4[:, 8:16, 16:32], r[3])
                vec.tensor_copy(w4[:, 16:24, 0:16], r[4])
                vec.tensor_scalar_mul(w4[:, 16:24, 16:32], r[6], 1.5 ** 0.5)
                vec.tensor_scalar_mul(vec_w[:], w2_in[:, 6, :, :], -(1.5 ** 0.5) / 3.0).then_inc(vec_w_ready, 1)
                dve.wait_ge(vec_w_ready, 1)
                vec.scalar_tensor_tensor(w2[:, 768:896].rearrange("h (w u) -> h w u", u=16), r[5], 3.0 ** -0.5,
                                         vec_w[:].rearrange("h u w -> h w u"), ALU.mult, ALU.add
                                         ).then_inc(weights_ready, 1)
            if layer == 3:
                dve.wait_ge(weights_in, 32)
                for k in range(2):
                    r = [w2_in[:, k, i, :, :].rearrange("h u w -> h w u") for i in range(4)]
                    w4 = w2[:, k, 0:128].rearrange("h (o u) -> h o u", u=16)
                    vec.tensor_copy(w4[:, :, 0:8], r[0])
                    vec.tensor_scalar_mul(w4[:, :, 8:16], r[1], 3.0 ** -0.5)
                    vec.tensor_copy(w2[:, k, 128:192].rearrange("h (o u) -> h o u", u=8), r[2])
                    last = vec.tensor_copy(w2[:, k, 192:256].rearrange("h (o u) -> h o u", u=8), r[3])
                last.then_inc(weights_ready, 1)
            dve.wait_ge(const2, 1)

            def body(g):
                s, s2 = g.slot(UNROLL), g.slot(2)
                done = [0]

                def link(ins):
                    done[0] += 1
                    ins.then_inc(v, 1)
                    dve.wait_ge(v, g.times(STEPS, done[0]))

                dve.wait_ge(loaded[s], g.turn(UNROLL) * LOADS + LOADS)
                link(vec.tensor_copy(idxf[:], idx[to][s][:]))
                wait_count(dve, sum_ready, g.times(1, -1))
                vec.tensor_tensor(same[s2][:], row[s][:], spread(idxf[:], [P, T, P], 2), ALU.is_equal
                                  ).then_inc(same_ready, 1)
                dve.wait_ge(same_ready, g.times(1, 1))
                link(vec.tensor_mul(earlier[:], same[s2][:], spread(before[:], [P, T, P], 1)))
                link(vec.tensor_reduce(repeat[:], earlier[:], AX.X, ALU.add))
                link(vec.tensor_scalar_min(repeat[:], repeat[:], 1.0))
                link(vec.tensor_scalar(earlier[:, :, 0], idxf[:], -1.0, trash[:, 0:1], ALU.mult, ALU.add))
                link(vec.tensor_mul(repeat[:], repeat[:], earlier[:, :, 0]))
                wait_count(dve, scattered[s2], g.turn(2) * SCATTERED)
                vec.tensor_add(slot_idx[s2][:], idxf[:], repeat[:]).then_inc(slot_ready, 1)
                dve.wait_ge(slot_ready, g.times(1, 1))
                if layer == 0:
                    vec.tensor_single_scalar(bits[:, 0, :], idx["src"][s][:], P - 1, ALU.bitwise_and)
                    link(vec.tensor_single_scalar(bits[:, 1, :], idx["src"][s][:], 7, ALU.logical_shift_right))
                    link(vec.tensor_copy(bitf[:], bits[:]))
                    vec.tensor_tensor(hot_lo[s2][:], spread(lo_row[:], [P, T, P], 1), spread(bitf[:, 0, :], [P, T, P], 2), ALU.is_equal)
                    vec.tensor_tensor(hot_hi[s2][:], spread(lo_row[:, 0:HI], [P, T, HI], 1), spread(bitf[:, 1, :], [P, T, HI], 2), ALU.is_equal)
                dve.wait_ge(gathered[s2], g.turn(2) * GATHERED + GATHERED)
                if layer == 0:
                    link(vec.tensor_add(got["src"][s2][:], got["src"][s2][:], attr["e32"][s][:]))
                    vec.tensor_scalar_max(msg[s2][:], got["src"][s2][:], 0.0).then_inc(msg_ready, 1)
                    dve.wait_ge(msg_ready, g.times(1, 1))
                    vec.sem_inc(got_used)
                    vec.sem_inc(load_used)
                if layer == 2:
                    vec.sem_inc(load_used)
                if layer == 1:
                    gs, gd, n3, wt = got["src"][s2], got["dst"][s2], attr["unit"][s], attr["weight"][s]
                    vec.tensor_copy(u32[:, :, 0:8], gs[:, :, 0:8])
                    vec.tensor_copy(u32[:, :, 8:16], gd[:, :, 0:8])
                    vec.tensor_copy(v16[:, :, 0:8, :].rearrange("p t u c -> p t (u c)"), gs[:, :, 8:32])
                    link(vec.tensor_copy(v16[:, :, 8:16, :].rearrange("p t u c -> p t (u c)"), gd[:, :, 8:32]))
                    link(vec.tensor_mul(dots[:], v16[:], spread(n3[:], [P, T, MUL1, 3], 2)))
                    link(vec.tensor_reduce(u32[:, :, 16:32], dots[:], AX.X, ALU.add))
                    for t in range(T):
                        b = (g.base * T + t) % 2
                        dve.wait_ge(w_mm, g.times(T, t + 1))
                        vec.tensor_mul(prod[:, t, :].rearrange("p (o u) -> p o u", u=32), p_w[b][:, 0:768].rearrange("p (o u) -> p o u", u=32),
                                       spread(u32[:, t, :], [P, 24, 32], 1))
                        vec.tensor_tensor(prodv[:, t, :].rearrange("p (k w u) -> p k w u", w=8, u=16),
                                          spread(p_w[b][:, 768:896].rearrange("p (w u) -> p w u", u=16), [P, 3, 8, 16], 1),
                                          spread(v16[:, t, :, :].rearrange("p u k -> p k u"), [P, 3, 8, 16], 2), ALU.mult
                                          ).then_inc(w_used, 1)
                    dve.wait_ge(w_used, g.times(T, T))
                    vec.tensor_reduce(red[:], prod[:].rearrange("p t (o u) -> p t o u", u=32), AX.X, ALU.add).then_inc(red_ready, 1)
                    vec.tensor_scalar_mul(wn[:], wt[:, :, 0], TANH_GAIN)
                    link(vec.tensor_reduce(redv[:], prodv[:].rearrange("p t (o u) -> p t o u", u=16), AX.X, ALU.add))
                    for t in range(T):
                        ins = vec.tensor_mul(vout[:, t, :, :], spread(red[:, t, 16:24], [P, 8, 3], 2), spread(n3[:, t, :], [P, 8, 3], 1))
                    link(ins)
                    link(vec.tensor_add(vout[:], vout[:], redv[:].rearrange("p t (k w) -> p t w k", w=8)))
                    dve.wait_ge(gate_ready, g.times(1, 1))
                    link(vec.tensor_mul(gate[s2][:], gate[s2][:], spread(wn[:], [P, T, 16], 2)))
                    link(vec.tensor_mul(vout[:], vout[:], spread(gate[s2][:, :, 8:16], [P, T, 8, 3], 3)))
                    vec.tensor_copy(msg[s2][:, :, 0:8], gate[s2][:, :, 0:8])
                    vec.tensor_scalar_mul(msg[s2][:, :, 8:32], vout[:].rearrange("p t w k -> p t (w k)"), 0.25).then_inc(msg_ready, 1)
                    dve.wait_ge(msg_ready, g.times(1, 1))
                    vec.sem_inc(got_used)
                    vec.sem_inc(load_used)
                if layer == 3:
                    gs, sh = got["src"][s2], attr["e4"][s]
                    v8 = gs[:, :, 8:32].rearrange("p t (u k) -> p t u k", k=3)
                    vec.tensor_mul(x16[:, :, 0:8], gs[:, :, 0:8], sh[:, :, 0:1].to_broadcast([P, T, 8]))
                    vec.tensor_mul(sv[:].rearrange("p t k u -> p t u k"), v8, sh[:, :, 0:1].unsqueeze(3).to_broadcast([P, T, 8, 3]))
                    link(vec.tensor_mul(dots[:], v8, spread(sh[:, :, 1:4], [P, T, 8, 3], 2)))
                    link(vec.tensor_reduce(x16[:, :, 8:16], dots[:], AX.X, ALU.add))
                    dve.wait_ge(w_mm, g.times(1, 1))
                    pw = p_w[:, 0:1280].rearrange("p (t c) -> p t c", c=256)
                    vec.tensor_mul(prods[:].rearrange("p t (w u) -> p t w u", u=16), pw[:, :, 0:128].rearrange("p t (w u) -> p t w u", u=16),
                                   spread(x16[:], [P, T, 8, 16], 2))
                    vec.tensor_mul(prodt[:].rearrange("p t (w u) -> p t w u", u=8), pw[:, :, 128:192].rearrange("p t (w u) -> p t w u", u=8),
                                   spread(gs[:, :, 0:8], [P, T, 8, 8], 2))
                    for t in range(T):
                        ins = vec.tensor_tensor(prodv[:, 3 * t:3 * t + 3, :].rearrange("p k (w u) -> p k w u", u=8),
                                                spread(pw[:, t, 192:256].rearrange("p (w u) -> p w u", u=8), [P, 3, 8, 8], 1),
                                                spread(sv[:, t, :, :], [P, 3, 8, 8], 2), ALU.mult)
                    ins.then_inc(w_used, 1)
                    dve.wait_ge(w_used, g.times(1, 1))
                    vec.tensor_reduce(msg[s2][:, :, 0:8], prods[:].rearrange("p t (w u) -> p t w u", u=16), AX.X, ALU.add)
                    vec.tensor_reduce(rt[:], prodt[:].rearrange("p t (w u) -> p t w u", u=8), AX.X, ALU.add)
                    link(vec.tensor_reduce(rv[:], prodv[:].rearrange("p t (w u) -> p t w u", u=8), AX.X, ALU.add))
                    for t in range(T):
                        ins = vec.tensor_mul(vout[:, t, :, :], spread(rt[:, t, :], [P, 8, 3], 2), spread(sh[:, t, 1:4], [P, 8, 3], 1))
                    link(ins)
                    vec.tensor_add(msg[s2][:, :, 8:32].rearrange("p t (w k) -> p t w k", k=3), vout[:],
                                   rv[:].rearrange("p (t k) w -> p t w k", k=3)).then_inc(msg_ready, 1)
                    dve.wait_ge(msg_ready, g.times(1, 1))
                    vec.sem_inc(got_used)
                    vec.sem_inc(load_used)
                assert done[0] == STEPS, (layer, done[0])

            groups(dve, body)
            if layer == 0:
                dve.wait_ge(deg_ready, 1)
                vec.tensor_copy(deg_sb[:], p_deg[:]).then_inc(deg_copied, 1)

        @block.tensor
        def _(pe):
            def sum_repeats(g):
                s2 = g.slot(2)
                pe.wait_ge(same_ready, g.times(1, 1))
                if layer == 2:
                    pe.wait_ge(gathered[s2], g.turn(2) * GATHERED + GATHERED)
                else:
                    pe.wait_ge(msg_ready, g.times(1, 1))
                wait_count(pe, summed_ready, g.times(1))
                if layer == 0:
                    for t in range(T):
                        nc.tensor.matmul(p_deg[:], hot_hi[s2][:, t, :], hot_lo[s2][:, t, :],
                                         start=False, stop=False, skip_group_check=True)
                for t in range(T):
                    last = nc.tensor.matmul(p_sum[:, t, :], same[s2][:, t, :], msg[s2][:, t, :], start=True, stop=True)
                last.then_inc(sum_ready, 1)

            def body(g):
                s, s2 = g.slot(UNROLL), g.slot(2)
                if layer == 1:
                    pe.wait_ge(loaded[s], g.turn(UNROLL) * LOADS + LOADS)
                    wait_count(pe, ht_ready, g.times(1))
                    pe.nop(nofuse=True)
                    for c0, c1 in ((0, 512), (512, GE)):
                        last = nc.tensor.matmul(p_h[:, c0:c1], w1[:], embt[s][:, c0:c1], start=True, stop=True)
                    last.then_inc(h_mm, 1)
                    pe.wait_ge(ht_ready, g.times(1, 1))
                    for t in range(T):
                        if t == 2 and g.base >= 1:
                            sum_repeats(Group(g.base - 1, g.i))
                        b = (g.base * T + t) % 2
                        wait_count(pe, w_used, g.times(T, t - 1))
                        for c0, c1 in ((0, 512), (512, 896)):
                            last = nc.tensor.matmul(p_w[b][:, c0:c1], ht[s2][:, t * P:(t + 1) * P], w2[:, c0:c1],
                                                    start=True, stop=True)
                        last.then_inc(w_mm, 1)
                elif layer == 3:
                    pe.wait_ge(loaded[s], g.turn(UNROLL) * LOADS + LOADS)
                    wait_count(pe, ht_ready, g.times(1))
                    pe.nop(nofuse=True)
                    for k in range(2):
                        for c0, c1 in ((0, 512), (512, GE)):
                            last = nc.tensor.matmul(p_h[k][:, c0:c1], w1[:, k * P:(k + 1) * P], embt[s][:, c0:c1], start=True, stop=True)
                    last.then_inc(h_mm, 1)
                    if g.base >= 1:
                        sum_repeats(Group(g.base - 1, g.i))
                    pe.wait_ge(ht_ready, g.times(1, 1))
                    wait_count(pe, w_used, g.times(1))
                    for t in range(T):
                        for k in range(2):
                            last = nc.tensor.matmul(p_w[:, t * 256:(t + 1) * 256], ht[s2][:, k, t * P:(t + 1) * P], w2[:, k, :],
                                                    start=k == 0, stop=k == 1)
                    last.then_inc(w_mm, 1)
                else:
                    sum_repeats(g)

            if emb:
                pe.wait_ge(weights_ready, 1)
            if layer == 0:
                pe.wait_ge(zero_ready, 1)
                nc.tensor.matmul(p_deg[:], no_hot[:, 0:HI], no_hot[:], start=True, stop=False, skip_group_check=True)
            groups(pe, body)
            if emb:
                sum_repeats(Group(G - 1))
            if layer == 0:
                nc.tensor.matmul(p_deg[:], no_hot[:, 0:HI], no_hot[:], start=False, stop=True, skip_group_check=True
                                 ).then_inc(deg_ready, 1)

        @block.scalar
        def _(act):
            def copy_sums(g):
                s2 = g.slot(2)
                act.wait_ge(sum_ready, g.times(1, 1))
                wait_count(act, scattered[s2], g.turn(2) * SCATTERED)
                ins = nc.scalar.copy(summed[s2][:], p_sum[:])
                ins.then_inc(summed_ready, 1)

            def body(g):
                s2 = g.slot(2)
                if layer == 1:
                    act.wait_ge(h_mm, g.times(1, 1))
                    wait_count(act, w_mm, g.times(T, -T))
                    nc.scalar.activation(ht[s2][:], p_h[:, 0:GE], ACT.Relu,
                                         scale=0.2 ** 0.5 / 4.0).then_inc(ht_ready, 1)
                    if g.base >= 1:
                        copy_sums(Group(g.base - 1, g.i))
                    act.wait_ge(red_ready, g.times(1, 1))
                    wait_count(act, msg_ready, g.times(1, -1))
                    nc.scalar.activation(gate[s2][:], red[:, :, 0:16], ACT.Tanh, scale=1.0 / 32 ** 0.5).then_inc(gate_ready, 1)
                elif layer == 3:
                    act.wait_ge(h_mm, g.times(1, 1))
                    wait_count(act, w_mm, g.times(1, -1))
                    for k in range(2):
                        last = nc.scalar.activation(ht[s2][:, k, :], p_h[k][:, 0:GE], ACT.Relu,
                                                    scale=0.5 / 16.0 * (1.0 / 128.0) ** 0.5 / (E / N) ** 0.5)
                    last.then_inc(ht_ready, 1)
                    if g.base >= 1:
                        copy_sums(Group(g.base - 1, g.i))
                else:
                    copy_sums(g)

            groups(act, body)
            if emb:
                copy_sums(Group(G - 1))


DEPTH = 4
WARM = (G - DEPTH - UNROLL) % UNROLL + DEPTH + UNROLL


def pipeline(eng, body):
    def plain(step):
        return lambda k: Group(step - k) if 0 <= step - k < G else None

    for step in range(WARM):
        body(plain(step))
    with eng.Fori(0, (G - WARM) // UNROLL) as i:
        for c in range(UNROLL):
            body(lambda k, c=c: Group(WARM + c - k, i))
    for step in range(G, G + DEPTH):
        body(plain(step))


assert (G - WARM) % UNROLL == 0 and WARM > DEPTH + UNROLL


def done(eng, sem, g):
    eng.wait_ge(sem, g.times(1, 1))


def free(eng, sem, g, slots):
    wait_count(eng, sem, g.times(1, 1 - slots))


def arrived(eng, sems, g, adds):
    eng.wait_ge(sems[g.slot(len(sems))], g.turn(len(sems)) * adds + adds)


def fetched(eng, sems, g, adds, slots):
    n = len(sems)
    wait_count(eng, sems[g.slot(n)], g.turn(n) * adds - adds * (slots // n - 1))


def window_setup(nc, a):
    with ExitStack() as ctx:
        sem = Sems(nc, "win")
        sb = lambda name, shape, dt=F32: ctx.enter_context(nc.sbuf_tensor(f"win_{name}", shape, dt))
        GP = G // NP
        dst = sb("dst", [NP, GP, GE], I32)
        row = sb("row", [NP, GP, GE], I32)
        low = sb("low", [NP, GP])
        high = sb("high", [NP, GP])
        low_i = sb("low_i", [NP, GP], I32)
        negrel = sb("negrel", [NP, GP, GE])
        rel_row = sb("rel_row", [NP, GP, GE], BF16)
        spans = sb("spans", [1, G])
        widest = sb("widest", [1, 1])
        dst_in, v, out, back, flag_ready = (sem(n) for n in ("dst_in", "v", "out", "back", "flag_ready"))
        block = ctx.enter_context(nc.Block())

        @block.sync
        def _(sp):
            sp.dma_start(dst[:].rearrange("p g e -> p (g e)"), a["dst"].rearrange("(p g) q t -> p (g q t)", p=NP)).then_inc(dst_in, 16)
            sp.dma_start(row[:].rearrange("p g e -> p (g e)"), a["dst_row"].rearrange("(p g) e -> p (g e)", p=NP)).then_inc(dst_in, 16)
            sp.wait_ge(v, 6)
            sp.dma_start(a["negrel"].rearrange("(p g) q t -> p (g q t)", p=NP), negrel[:].rearrange("p g e -> p (g e)")).then_inc(out, 16)
            sp.dma_start(a["rel_row"].rearrange("(p g) e -> p (g e)", p=NP), rel_row[:].rearrange("p g e -> p (g e)")).then_inc(out, 16)
            sp.dma_start(a["base"].rearrange("(p g) o -> p (g o)", p=NP), low_i[:]).then_inc(out, 16)
            sp.dma_start(a["span"].rearrange("(p g) o -> p (g o)", p=NP), high[:]).then_inc(out, 16)
            sp.wait_ge(out, 64)
            sp.dma_start(a["base_sb"][:], a["base"].rearrange("g o -> o g")).then_inc(back, 16)
            sp.dma_start(spans[:], a["span"].rearrange("g o -> o g")).then_inc(back, 16)
            sp.wait_ge(back, 32)
            sp.wait_ge(flag_ready, 1)

        @block.vector
        def _(dve):
            vec = nc.vector
            dve.wait_ge(dst_in, 32)
            vec.tensor_reduce(low[:], dst[:], AX.X, ALU.min).then_inc(v, 1)
            vec.tensor_reduce(high[:], dst[:], AX.X, ALU.max).then_inc(v, 1)
            dve.wait_ge(v, 2)
            vec.tensor_copy(low_i[:], low[:]).then_inc(v, 1)
            vec.tensor_sub(high[:], high[:], low[:]).then_inc(v, 1)
            vec.tensor_tensor(negrel[:], spread(low[:], [NP, GP, GE], 2), dst[:], ALU.subtract).then_inc(v, 1)
            vec.tensor_tensor(rel_row[:], row[:], spread(low[:], [NP, GP, GE], 2), ALU.subtract).then_inc(v, 1)
            dve.wait_ge(back, 32)
            vec.tensor_reduce(widest[:], spans[:], AX.X, ALU.max).then_inc(v, 1)
            dve.wait_ge(v, 7)
            vec.tensor_single_scalar(a["flag_sb"][:], widest[:], float(WIN), ALU.is_lt).then_inc(flag_ready, 1)
    sem.clear()


def window_sums(nc, a, layer):
    with ExitStack() as ctx:
        sem = a["sems"][layer]
        p_all = ctx.enter_context(nc.psum_tensor(f"f{layer}_sums", [NP, NJ * D], F32))
        turned, copied = sem("turned"), sem("copied")
        block = ctx.enter_context(nc.Block())

        @block.tensor
        def _(pe):
            nodes = a["acc_t"][:, 0:N].rearrange("d (p j) -> d p j", j=NJ)
            for j in range(NJ):
                last = nc.tensor.matmul(p_all[:, j * D:(j + 1) * D], nodes[:, :, j], a["ident"][0:D, 0:D], start=True, stop=True)
            last.then_inc(turned, 1)

        @block.vector
        def _(dve):
            dve.wait_ge(turned, 1)
            nc.vector.tensor_copy(a["sums_sb"][:], p_all[:]).then_inc(copied, 1)
            dve.wait_ge(copied, 1)


def table_sums(nc, a, layer):
    with ExitStack() as ctx:
        sem = a["sems"][layer]
        parts = [a["sums_sb"]] + [ctx.enter_context(nc.sbuf_tensor(f"t{layer}_sums{t}", [NP, NJ * D], F32)) for t in range(1, T)]
        sums_in, summed = sem("sums_in"), sem("summed")
        block = ctx.enter_context(nc.Block())

        @block.sync
        def _(sp):
            for t in range(T):
                sp.dma_start(parts[t][:], a["acc"][layer][t][0:N, :].rearrange("(p j) d -> p (j d)", p=NP)).then_inc(sums_in, 16)

        @block.vector
        def _(dve):
            dve.wait_ge(sums_in, 16 * T)
            for t in range(1, T):
                nc.vector.tensor_add(parts[0][:], parts[0][:], parts[t][:]).then_inc(summed, 1)
                dve.wait_ge(summed, t)


def clear_tables(nc, a, layer):
    with ExitStack() as ctx:
        sem = a["sems"][layer]
        zeros = ctx.enter_context(nc.sbuf_tensor(f"z{layer}_zeros", [P, NJ * D], F32))
        zeroed, zero_out = sem("zeroed"), sem("zero_out")
        block = ctx.enter_context(nc.Block())

        @block.gpsimd
        def _(pool):
            pool.memset(zeros[:], 0.0).then_inc(zeroed, 1)

        @block.sync
        def _(sp):
            sp.wait_ge(zeroed, 1)
            for rows in a["acc"][layer]:
                sp.dma_start(rows[0:N, :].rearrange("(p r) d -> p (r d)", p=NP), zeros[0:NP, :]).then_inc(zero_out, 16)
                sp.dma_start(rows[N:N + TRASH, :], zeros[0:TRASH, 0:D]).then_inc(zero_out, 16)
            sp.wait_ge(zero_out, 32 * T)


class WindowPass:

    def __init__(self, nc, a, layer, sb, ps, p_acc=None):
        self.nc, self.a, sem = nc, a, a["sems"][layer]
        self.dist = [sb(f"dist{s}", [P, T, WIN]) for s in range(2)]
        self.hot = [sb(f"hot{s}", [P, T, WIN]) for s in range(2)]
        self.p_acc = ps("p_acc", [D, WIN])[:] if p_acc is None else p_acc
        self.dist_ready, self.hot_ready, self.acc_ready, self.acc_added = (
            sem(n) for n in ("dist_ready", "hot_ready", "acc_ready", "acc_added"))

    def one_hot(self, act, g, negrel):
        dist = self.dist[g.slot(2)]
        free(act, self.hot_ready, g, 2)
        for t in range(T):
            last = self.nc.scalar.activation(dist[:, t, :], self.a["row_iota"][:], ACT.Abs, bias=negrel[:, t:t + 1])
        last.then_inc(self.dist_ready, 1)
        done(act, self.dist_ready, g)
        free(act, self.acc_ready, g, 2)
        self.nc.scalar.activation(self.hot[g.slot(2)][:], dist[:], ACT.Relu, scale=-1.0, bias=1.0).then_inc(self.hot_ready, 1)

    def sum_window(self, pe, g, msg, msg_ready):
        done(pe, self.hot_ready, g)
        done(pe, msg_ready, g)
        free(pe, self.acc_added, g, 1)
        pe.nop(nofuse=True)
        for t in range(T):
            last = self.nc.tensor.matmul(self.p_acc, msg[:, t, :], self.hot[g.slot(2)][:, t, :], start=t == 0, stop=t == T - 1)
        last.then_inc(self.acc_ready, 1)

    def add_window(self, dve, g):
        base = dve.value_load(self.a["base_sb"][0:1, bass.ds(g.times(1), 1)], min_val=0, max_val=N - 1)
        done(dve, self.acc_ready, g)
        free(dve, self.acc_added, g, 1)
        nodes = self.a["acc_t"][:, bass.ds(base, WIN)]
        self.nc.vector.tensor_add(nodes, nodes, self.p_acc).then_inc(self.acc_added, 1)


def tensors(nc, ctx, prefix):
    return (lambda name, shape, dt=F32: ctx.enter_context(nc.sbuf_tensor(f"{prefix}_{name}", shape, dt)),
            lambda name, shape, dt=F32: ctx.enter_context(nc.psum_tensor(f"{prefix}_{name}", shape, dt)))


def window_pass_0(nc, a):
    LOADS, GATHERED = 16 * 3, 16 * T
    with ExitStack() as ctx:
        sem = a["sems"][0]
        sb, ps = tensors(nc, ctx, "w0")
        w = WindowPass(nc, a, 0, sb, ps)
        idx = [sb(f"idx{s}", [P, T], I32) for s in range(UNROLL)]
        edge = [sb(f"edge{s}", [P, T, D]) for s in range(UNROLL)]
        negrel = [sb(f"negrel{s}", [P, T]) for s in range(UNROLL)]
        rows = [sb(f"rows{s}", [P, T, D]) for s in range(2)]
        msg = [sb(f"msg{s}", [P, T, D]) for s in range(2)]
        bits = sb("bits", [P, 2, T], I32)
        bitf = sb("bitf", [P, 2, T])
        hot_lo = [sb(f"hot_lo{s}", [P, T, P], BF16) for s in range(2)]
        hot_hi = [sb(f"hot_hi{s}", [P, T, HI], BF16) for s in range(2)]
        no_hot = sb("no_hot", [P, P], BF16)
        deg_sb = sb("deg_sb", [HI, P])
        p_deg = ps("p_deg", [HI, P])
        loaded = [sem(f"loaded{s}") for s in range(UNROLL)]
        gathered = [sem(f"gathered{s}") for s in range(2)]
        bits_ready, bitf_ready, deg_hot_ready, added, msg_ready, zero_ready, deg_ready, deg_copied, deg_out = (
            sem(n) for n in ("bits_ready", "bitf_ready", "deg_hot_ready", "added", "msg_ready", "zero_ready",
                             "deg_ready", "deg_copied", "deg_out"))
        block = ctx.enter_context(nc.Block())

        @block.sync
        def _(sp):
            def step(at):
                if g := at(0):
                    s, k = g.slot(UNROLL), g.times(1)
                    fetched(sp, gathered, g, GATHERED, UNROLL)
                    sp.nop(nofuse=True)
                    free(sp, msg_ready, g, UNROLL)
                    free(sp, w.hot_ready, g, UNROLL)
                    sp.dma_start(idx[s][:], pick(a["src"], k)).then_inc(loaded[s], 16)
                    sp.dma_start(edge[s][:].rearrange("p t d -> p (t d)"), pick(a["e32"], k)).then_inc(loaded[s], 16)
                    sp.dma_start(negrel[s][:], pick(a["negrel"], k)).then_inc(loaded[s], 16)

            pipeline(sp, step)
            sp.wait_ge(deg_copied, 1)
            sp.dma_start(a["deg"].rearrange("(h l) o -> h (l o)", l=P), deg_sb[:]).then_inc(deg_out, 16)
            sp.wait_ge(deg_out, 16)

        @block.gpsimd
        def _(pool):
            pool.memset(no_hot[:], 0.0).then_inc(zero_ready, 1)

            def step(at):
                if g := at(0):
                    s2 = g.slot(2)
                    free(pool, msg_ready, g, 2)
                    pool.nop(nofuse=True)
                    arrived(pool, loaded, g, LOADS)
                    pool.nop(nofuse=True)
                    gather_rows(pool, a["table"][0], idx[g.slot(UNROLL)], rows[s2], gathered[s2])

            pipeline(pool, step)

        @block.vector
        def _(dve):
            vec = nc.vector

            def step(at):
                if g := at(1):
                    s, s2 = g.slot(UNROLL), g.slot(2)
                    arrived(dve, loaded, g, LOADS)
                    vec.tensor_single_scalar(bits[:, 0, :], idx[s][:], P - 1, ALU.bitwise_and)
                    vec.tensor_single_scalar(bits[:, 1, :], idx[s][:], 7, ALU.logical_shift_right).then_inc(bits_ready, 1)
                    done(dve, bits_ready, g)
                    vec.tensor_copy(bitf[:], bits[:]).then_inc(bitf_ready, 1)
                    done(dve, bitf_ready, g)
                    free(dve, w.acc_ready, g, 2)
                    vec.tensor_tensor(hot_lo[s2][:], spread(a["row_iota"][:], [P, T, P], 1),
                                      spread(bitf[:, 0, :], [P, T, P], 2), ALU.is_equal)
                    vec.tensor_tensor(hot_hi[s2][:], spread(a["row_iota"][:, 0:HI], [P, T, HI], 1),
                                      spread(bitf[:, 1, :], [P, T, HI], 2), ALU.is_equal).then_inc(deg_hot_ready, 1)
                    arrived(dve, gathered, g, GATHERED)
                    vec.tensor_add(rows[s2][:], rows[s2][:], edge[s][:]).then_inc(added, 1)
                    done(dve, added, g)
                    vec.tensor_scalar_max(msg[s2][:], rows[s2][:], 0.0).then_inc(msg_ready, 1)
                if g := at(2):
                    w.add_window(dve, g)

            pipeline(dve, step)
            dve.wait_ge(deg_ready, 1)
            vec.tensor_copy(deg_sb[:], p_deg[:]).then_inc(deg_copied, 1)

        @block.scalar
        def _(act):
            def step(at):
                if g := at(1):
                    arrived(act, loaded, g, LOADS)
                    w.one_hot(act, g, negrel[g.slot(UNROLL)])

            pipeline(act, step)

        @block.tensor
        def _(pe):
            pe.wait_ge(zero_ready, 1)
            nc.tensor.matmul(p_deg[:], no_hot[:, 0:HI], no_hot[:], start=True, stop=False, skip_group_check=True)

            def step(at):
                if g := at(1):
                    s2 = g.slot(2)
                    done(pe, deg_hot_ready, g)
                    for t in range(T):
                        nc.tensor.matmul(p_deg[:], hot_hi[s2][:, t, :], hot_lo[s2][:, t, :], start=False, stop=False, skip_group_check=True)
                    w.sum_window(pe, g, msg[s2], msg_ready)

            pipeline(pe, step)
            nc.tensor.matmul(p_deg[:], no_hot[:, 0:HI], no_hot[:], start=False, stop=True, skip_group_check=True).then_inc(deg_ready, 1)


def gather_rows(pool, table, idx, rows, sem):
    for t in range(T):
        pool.indirect_dma_start(out=rows[:, t, :], out_offset=None, in_=table[0:N, :],
                                in_offset=bass.IndirectOffsetOnAxis(ap=idx[:, t:t + 1], axis=0)).then_inc(sem, 16)


def load_weights_3(nc, w2_in, w2):
    vec = nc.vector
    for k in range(2):
        r = [w2_in[:, k, i, :, :].rearrange("h u w -> h w u") for i in range(4)]
        w4 = w2[:, k, 0:128].rearrange("h (o u) -> h o u", u=16)
        vec.tensor_copy(w4[:, :, 0:8], r[0])
        vec.tensor_scalar_mul(w4[:, :, 8:16], r[1], 3.0 ** -0.5)
        vec.tensor_copy(w2[:, k, 128:192].rearrange("h (o u) -> h o u", u=8), r[2])
        last = vec.tensor_copy(w2[:, k, 192:256].rearrange("h (o u) -> h o u", u=8), r[3])
    return last


def window_pass_3(nc, a):
    LOADS, GATHERED = 16 * 4, 16 * T
    BANKS = ((0, 2), (2, 4), (4, T))
    with ExitStack() as ctx:
        sem = a["sems"][3]
        sb, ps = tensors(nc, ctx, "w3")
        w = WindowPass(nc, a, 3, sb, ps)
        idx = [sb(f"idx{s}", [P, T], I32) for s in range(UNROLL)]
        harm = [sb(f"harm{s}", [P, T, 4]) for s in range(UNROLL)]
        embt = [sb(f"embt{s}", [EMB3, GE]) for s in range(UNROLL)]
        negrel = [sb(f"negrel{s}", [P, T]) for s in range(UNROLL)]
        rows = [sb(f"rows{s}", [P, T, D]) for s in range(UNROLL)]
        msg = [sb(f"msg{s}", [P, T, D]) for s in range(2)]
        w1 = sb("w1", [EMB3, HID3])
        w2_in = sb("w2_in", [P, 2, 4, MUL3, MUL3])
        w2 = sb("w2", [P, 2, 256])
        ht = [sb(f"ht{s}", [P, 2, GE]) for s in range(2)]
        x16 = sb("x16", [P, T, 16])
        sv = sb("sv", [P, T, 3, MUL3])
        dots = sb("dots", [P, T, MUL3, 3])
        prods = sb("prods", [P, T, 128])
        prodt = sb("prodt", [P, T, 64])
        prodv = sb("prodv", [P, T * 3, 64])
        rt = sb("rt", [P, T, 8])
        rv = sb("rv", [P, T * 3, 8])
        vout = sb("vout", [P, T, 8, 3])
        p_h = [ps(f"p_h{k}", [P, 1024]) for k in range(2)]
        p_w = ps("p_w", [P, 3 * 512])
        loaded = [sem(f"loaded{s}") for s in range(UNROLL)]
        gathered = [sem(f"gathered{s}") for s in range(UNROLL)]
        dots_ready, x_ready, w_used, red_ready, vout_ready, msg_ready, h_mm, ht_ready, w_mm, weights_in, weights_ready = (
            sem(n) for n in ("dots_ready", "x_ready", "w_used", "red_ready", "vout_ready", "msg_ready", "h_mm", "ht_ready",
                             "w_mm", "weights_in", "weights_ready"))
        block = ctx.enter_context(nc.Block())

        @block.sync
        def _(sp):
            sp.dma_start(w1[:], a["w1_3"]).then_inc(weights_in, 16)
            sp.dma_start(w2_in[:], a["w2_3"]).then_inc(weights_in, 16)

            def step(at):
                if g := at(0):
                    s, k = g.slot(UNROLL), g.times(1)
                    fetched(sp, gathered, g, GATHERED, UNROLL)
                    sp.nop(nofuse=True)
                    free(sp, msg_ready, g, UNROLL)
                    free(sp, w.hot_ready, g, UNROLL)
                    free(sp, h_mm, g, UNROLL)
                    sp.dma_start(idx[s][:], pick(a["src"], k)).then_inc(loaded[s], 16)
                    sp.dma_start(harm[s][:].rearrange("p t d -> p (t d)"), pick(a["e4"], k)).then_inc(loaded[s], 16)
                    sp.dma_start(embt[s][:], pick(a["emb3"], k)).then_inc(loaded[s], 16)
                    sp.dma_start(negrel[s][:], pick(a["negrel"], k)).then_inc(loaded[s], 16)

            pipeline(sp, step)

        @block.gpsimd
        def _(pool):
            def step(at):
                if g := at(0):
                    s = g.slot(UNROLL)
                    free(pool, msg_ready, g, UNROLL)
                    pool.nop(nofuse=True)
                    arrived(pool, loaded, g, LOADS)
                    pool.nop(nofuse=True)
                    gather_rows(pool, a["table"][3], idx[s], rows[s], gathered[s])

            pipeline(pool, step)

        @block.vector
        def _(dve):
            vec = nc.vector
            dve.wait_ge(weights_in, 32)
            load_weights_3(nc, w2_in, w2).then_inc(weights_ready, 1)

            def step(at):
                if g := at(2):
                    s2 = g.slot(2)
                    gs, sh = rows[g.slot(UNROLL)], harm[g.slot(UNROLL)]
                    arrived(dve, loaded, g, LOADS)
                    arrived(dve, gathered, g, GATHERED)
                    free(dve, msg_ready, g, 1)
                    v8 = gs[:, :, 8:32].rearrange("p t (u k) -> p t u k", k=3)
                    vec.tensor_mul(dots[:], v8, spread(sh[:, :, 1:4], [P, T, 8, 3], 2)).then_inc(dots_ready, 1)
                    vec.tensor_mul(x16[:, :, 0:8], gs[:, :, 0:8], sh[:, :, 0:1].to_broadcast([P, T, 8]))
                    vec.tensor_mul(sv[:].rearrange("p t k u -> p t u k"), v8, sh[:, :, 0:1].unsqueeze(3).to_broadcast([P, T, 8, 3]))
                    done(dve, dots_ready, g)
                    vec.tensor_reduce(x16[:, :, 8:16], dots[:], AX.X, ALU.add).then_inc(x_ready, 1)
                    done(dve, x_ready, g)
                    for b, (t0, t1) in enumerate(BANKS):
                        n, pw = t1 - t0, p_w[:, t0 * 256:t1 * 256].rearrange("p (t c) -> p t c", c=256)
                        dve.wait_ge(w_mm, g.times(len(BANKS), b + 1))
                        vec.tensor_mul(prods[:, t0:t1, :].rearrange("p t (w u) -> p t w u", u=16),
                                       pw[:, :, 0:128].rearrange("p t (w u) -> p t w u", u=16), spread(x16[:, t0:t1, :], [P, n, 8, 16], 2))
                        vec.tensor_mul(prodt[:, t0:t1, :].rearrange("p t (w u) -> p t w u", u=8),
                                       pw[:, :, 128:192].rearrange("p t (w u) -> p t w u", u=8), spread(gs[:, t0:t1, 0:8], [P, n, 8, 8], 2))
                        for t in range(t0, t1):
                            last = vec.tensor_mul(prodv[:, 3 * t:3 * t + 3, :].rearrange("p k (w u) -> p k w u", u=8),
                                                  spread(pw[:, t - t0, 192:256].rearrange("p (w u) -> p w u", u=8), [P, 3, 8, 8], 1),
                                                  spread(sv[:, t, :, :], [P, 3, 8, 8], 2))
                        last.then_inc(w_used, 1)
                    dve.wait_ge(w_used, g.times(len(BANKS), len(BANKS)))
                    free(dve, w.acc_ready, g, 2)
                    vec.tensor_reduce(rt[:], prodt[:].rearrange("p t (w u) -> p t w u", u=8), AX.X, ALU.add)
                    vec.tensor_reduce(rv[:], prodv[:].rearrange("p t (w u) -> p t w u", u=8), AX.X, ALU.add).then_inc(red_ready, 1)
                    vec.tensor_reduce(msg[s2][:, :, 0:8], prods[:].rearrange("p t (w u) -> p t w u", u=16), AX.X, ALU.add)
                    done(dve, red_ready, g)
                    vec.tensor_mul(vout[:], spread(rt[:], [P, T, 8, 3], 3), spread(sh[:, :, 1:4], [P, T, 8, 3], 2)).then_inc(vout_ready, 1)
                if g := at(3):
                    w.add_window(dve, g)
                if g := at(2):
                    done(dve, vout_ready, g)
                    vec.tensor_add(msg[g.slot(2)][:, :, 8:32].rearrange("p t (w k) -> p t w k", k=3), vout[:],
                                   rv[:].rearrange("p (t k) w -> p t w k", k=3)).then_inc(msg_ready, 1)

            pipeline(dve, step)

        @block.scalar
        def _(act):
            def step(at):
                if g := at(1):
                    s2 = g.slot(2)
                    done(act, h_mm, g)
                    wait_count(act, w_mm, g.times(len(BANKS), -len(BANKS)))
                    for k in range(2):
                        last = nc.scalar.activation(ht[s2][:, k, :], p_h[k][:, 0:GE], ACT.Relu,
                                                    scale=0.5 / 16.0 * (1.0 / 128.0) ** 0.5 / (E / N) ** 0.5)
                    last.then_inc(ht_ready, 1)
                if g := at(2):
                    arrived(act, loaded, g, LOADS)
                    w.one_hot(act, g, negrel[g.slot(UNROLL)])

            pipeline(act, step)

        @block.tensor
        def _(pe):
            pe.wait_ge(weights_ready, 1)

            def step(at):
                if g := at(1):
                    s = g.slot(UNROLL)
                    arrived(pe, loaded, g, LOADS)
                    free(pe, ht_ready, g, 1)
                    for k in range(2):
                        for c0, c1 in ((0, 512), (512, GE)):
                            last = nc.tensor.matmul(p_h[k][:, c0:c1], w1[:, k * P:(k + 1) * P], embt[s][:, c0:c1], start=True, stop=True)
                    last.then_inc(h_mm, 1)
                if g := at(2):
                    done(pe, ht_ready, g)
                    for bank, (t0, t1) in enumerate(BANKS):
                        wait_count(pe, w_used, g.times(len(BANKS), bank + 1 - len(BANKS)))
                        for t in range(t0, t1):
                            for k in range(2):
                                last = nc.tensor.matmul(p_w[:, t * 256:(t + 1) * 256], ht[g.slot(2)][:, k, t * P:(t + 1) * P], w2[:, k, :],
                                                        start=k == 0, stop=k == 1)
                        last.then_inc(w_mm, 1)
                if g := at(3):
                    w.sum_window(pe, g, msg[g.slot(2)], msg_ready)

            pipeline(pe, step)


class WindowGather:

    def __init__(self, nc, a, layer, sb, ps, p_rows=None):
        self.nc, self.a, self.layer, sem = nc, a, layer, a["sems"][layer]
        self.rel_row = [sb(f"rel_row{s}", [P, GE], BF16) for s in range(UNROLL)]
        self.nodes = [sb(f"nodes{s}", [WIN, 3 * D], BF16) for s in range(UNROLL)]
        self.hot = [sb(f"hot_t{s}", [WIN, GE], BF16) for s in range(2)]
        self.p_rows = ps("p_rows", [P, T, D])[:] if p_rows is None else p_rows
        self.hot_ready, self.rows_ready = sem("hot_t_ready"), sem("rows_ready")

    def load(self, sp, g, sem):
        s, k = g.slot(UNROLL), g.times(1)
        sp.nop(nofuse=True)
        base = sp.value_load(self.a["base_sb"][0:1, bass.ds(k, 1)], min_val=0, max_val=N - 1)
        sp.dma_start(self.rel_row[s][:], self.a["rel_row"][bass.ds(k, 1), :].to_broadcast([P, GE])).then_inc(sem, 16)
        sp.dma_start(self.nodes[s][:], self.a["split"][self.layer][bass.ds(base, WIN), :]).then_inc(sem, 16)

    def one_hot(self, dve, g):
        free(dve, self.rows_ready, g, 2)
        self.nc.vector.tensor_scalar(self.hot[g.slot(2)][:], self.rel_row[g.slot(UNROLL)][:], self.a["col_iota"][:, 0:1], None,
                                     ALU.is_equal).then_inc(self.hot_ready, 1)

    def product(self, pe, g):
        done(pe, self.hot_ready, g)
        nodes = self.nodes[g.slot(UNROLL)]
        for t in range(T):
            for part in range(3):
                last = self.nc.tensor.matmul(self.p_rows[:, t, :], self.hot[g.slot(2)][:, t * P:(t + 1) * P],
                                             nodes[:, part * D:(part + 1) * D], start=part == 0, stop=part == 2)
        last.then_inc(self.rows_ready, 1)


def window_pass_1(nc, a):
    LOADS_A, LOADS_B, GATHERED = 16 * 4, 16 * 3, 16 * T
    SGT, G_ROWS, T_AT = 40, 16, 32
    SPLIT = 3
    with ExitStack() as ctx:
        sem = a["sems"][1]
        sb, ps = tensors(nc, ctx, "w1")
        p_low = ps("p_low", [P, 512])
        p_rows = p_low[:, 0:T * D].rearrange("p (t d) -> p t d", d=D)
        w = WindowPass(nc, a, 1, sb, ps, p_low[0:D, T * D:T * D + WIN])
        p_out = p_low[:, T * D + WIN:T * (D + SGT) + WIN].rearrange("p (t o) -> p t o", o=SGT)
        wg = WindowGather(nc, a, 1, sb, ps, p_rows)
        p_wv = [ps(f"p_wv{s}", [P, P])[:] for s in range(2)]
        p_sgt = ps("p_sgt", [SGT, 4 * P])
        p_he = ps("p_he", [P, 1024])
        p_xt = p_he[0:SPLIT * 32, :]
        p_xe = [ps(f"p_xe{s}", [P, 512]) for s in range(2)]
        idx = [sb(f"idx{s}", [P, T], I32) for s in range(UNROLL)]
        embt = [sb(f"embt{s}", [EMB1, GE]) for s in range(UNROLL)]
        unit = [sb(f"unit{s}", [P, T, 3]) for s in range(UNROLL)]
        weight = [sb(f"weight{s}", [P, T]) for s in range(UNROLL)]
        negrel = [sb(f"negrel{s}", [P, T]) for s in range(UNROLL)]
        rows = [sb(f"rows{s}", [P, T, D]) for s in range(2)]
        x32 = [sb(f"x32{s}", [P, T, 32]) for s in range(2)]
        v16 = [sb(f"v16{s}", [P, T, MUL1, 3]) for s in range(UNROLL)]
        dots = sb("dots", [P, T, MUL1, 3])
        dot2 = sb("dot2", [P, T, MUL1])
        xs = [sb(f"xs{s}", [P, T, SPLIT, 32], BF16) for s in range(2)]
        rest = [sb(f"rest{s}", [P, T, 32]) for s in range(2)]
        xt = [sb(f"xt{s}", [SPLIT * 32, GE], BF16) for s in range(2)]
        he = [sb(f"he{s}", [P, GE]) for s in range(UNROLL)]
        prod = [sb(f"prod{s}", [P, 4, P]) for s in range(2)]
        prodv = sb("prodv", [P, T, 24 * 16])
        redv = sb("redv", [P, T, 24])
        vout = sb("vout", [P, T, 8, 3])
        vsum = sb("vsum", [P, T, 8, 3])
        sgt = [sb(f"sgt{s}", [SGT, GE]) for s in range(2)]
        gate = [sb(f"gate{s}", [P, T, 16]) for s in range(2)]
        msg = [sb(f"msg{s}", [P, T, D]) for s in range(2)]
        w1 = sb("w1", [EMB1, 8, HID1])
        w2_in = sb("w2_in", [HID1, 7, MUL1, OUT1])
        w2_uh = sb("w2_uh", [P, 2, 7, OUT1])
        wc = sb("wc", [P, 4, SGT])
        vec_w = sb("vec_w", [HID1, MUL1, OUT1])
        vec_w2 = sb("vec_w2", [HID1, MUL1, OUT1])
        wv = sb("wv", [HID1, P])
        ident_b = sb("ident_b", [P, P], BF16)
        pick_f = sb("pick_f", [SPLIT * 32, 4, P])
        pick_b = sb("pick_b", [SPLIT * 32, 4, P], BF16)
        loaded_a = [sem(f"loaded_a{s}") for s in range(UNROLL)]
        loaded_b = [sem(f"loaded_b{s}") for s in range(UNROLL)]
        gathered = [sem(f"gathered{s}") for s in range(2)]
        (he_mm, he_ready, src_copied, dst_copied, dots_ready, dot2_ready, q_ready, high_ready, rest_ready, mid_ready, low_ready,
         xt_mm, xt_ready, xe_ready, prod_ready, sgt_tile, wv_ready, wv_used, redv_ready, vout_ready, vsum_ready, sgt_first, sgt_last, out_ready,
         gate_ready, gate_copied, msg_ready, weights_in, vec_w_ready, vec_w2_ready, weights_ready, picks, picks_ready, sgt_zeroed) = (
            sem(n) for n in ("he_mm", "he_ready", "src_copied", "dst_copied", "dots_ready", "dot2_ready", "q_ready", "high_ready",
                             "rest_ready", "mid_ready", "low_ready", "xt_mm", "xt_ready", "xe_ready", "prod_ready", "sgt_tile",
                             "wv_ready", "wv_used", "redv_ready", "vout_ready", "vsum_ready", "sgt_first", "sgt_last", "out_ready", "gate_ready",
                             "gate_copied", "msg_ready", "weights_in", "vec_w_ready", "vec_w2_ready", "weights_ready",
                             "picks", "picks_ready", "sgt_zeroed"))
        block = ctx.enter_context(nc.Block())

        @block.sync
        def _(sp):
            for u in range(8):
                sp.dma_start(w1[:, u, :], a["w1_1"]).then_inc(weights_in, 16)
            sp.dma_start(w2_in[:], a["w2_1"]).then_inc(weights_in, 16)
            sp.dma_start(w2_uh[:], a["w2_uh"]).then_inc(weights_in, 16)

            def step(at):
                if g := at(0):
                    s, k = g.slot(UNROLL), g.times(1)
                    fetched(sp, gathered, g, GATHERED, UNROLL)
                    sp.nop(nofuse=True)
                    free(sp, wg.rows_ready, g, UNROLL)
                    free(sp, he_mm, g, UNROLL)
                    wg.load(sp, g, loaded_a[s])
                    sp.dma_start(idx[s][:], pick(a["src"], k)).then_inc(loaded_a[s], 16)
                    sp.dma_start(embt[s][:], pick(a["emb1"], k)).then_inc(loaded_a[s], 16)
                if g := at(1):
                    s, k = g.slot(UNROLL), g.times(1)
                    free(sp, msg_ready, g, UNROLL)
                    free(sp, w.hot_ready, g, UNROLL)
                    sp.dma_start(unit[s][:].rearrange("p t c -> p (t c)"), pick(a["unit"], k)).then_inc(loaded_b[s], 16)
                    sp.dma_start(weight[s][:], pick(a["weight"], k)).then_inc(loaded_b[s], 16)
                    sp.dma_start(negrel[s][:], pick(a["negrel"], k)).then_inc(loaded_b[s], 16)

            pipeline(sp, step)

        @block.gpsimd
        def _(pool):
            pool.memset(pick_f[:], 0.0).then_inc(picks, 1)
            for s in range(2):
                pool.memset(sgt[s][:], 0.0).then_inc(sgt_zeroed, 1)
            for b in range(4):
                for part in range(SPLIT):
                    pool.wait_ge(picks, b * SPLIT + part + 1)
                    view = pick_f[:, b, :].rearrange("p (u h) -> p u h", h=HID1)
                    pool.affine_select(out=view, in_=view, compare_op=ALU.not_equal, fill=1.0, base=-(32 * part + 8 * b),
                                       pattern=[[-1, 8], [0, HID1]], channel_multiplier=1).then_inc(picks, 1)

            def step(at):
                if g := at(2):
                    s, s2 = g.slot(UNROLL), g.slot(2)
                    v = v16[s]
                    arrived(pool, loaded_b, g, LOADS_B)
                    done(pool, src_copied, g)
                    done(pool, dst_copied, g)
                    free(pool, q_ready, g, 1)
                    nc.gpsimd.tensor_mul(dots[:], v[:], spread(unit[s][:], [P, T, MUL1, 3], 2)).then_inc(dots_ready, 1)
                    done(pool, dots_ready, g)
                    nc.gpsimd.tensor_add(dot2[:], dots[:, :, :, 0], dots[:, :, :, 1]).then_inc(dot2_ready, 1)
                    done(pool, dot2_ready, g)
                    nc.gpsimd.tensor_add(x32[s2][:, :, 16:32], dot2[:], dots[:, :, :, 2]).then_inc(q_ready, 1)
                if g := at(0):
                    s2 = g.slot(2)
                    free(pool, src_copied, g, 2)
                    pool.nop(nofuse=True)
                    arrived(pool, loaded_a, g, LOADS_A)
                    pool.nop(nofuse=True)
                    gather_rows(pool, a["table"][1], idx[g.slot(UNROLL)], rows[s2], gathered[s2])

            pipeline(pool, step)

        @block.vector
        def _(dve):
            vec = nc.vector
            dve.wait_ge(weights_in, 160)
            for half in range(2):
                for o, (i_x, i_q) in enumerate(((0, 1), (2, 3))):
                    vec.tensor_copy(wc[:, half, 8 * o:8 * o + 8], w2_uh[:, half, i_x, :])
                    vec.tensor_copy(wc[:, 2 + half, 8 * o:8 * o + 8], w2_uh[:, half, i_q, :])
                vec.tensor_scalar_mul(wc[:, half, T_AT:SGT], w2_uh[:, half, 4, :], 0.25)
                vec.tensor_scalar_mul(wc[:, 2 + half, T_AT:SGT], w2_uh[:, half, 6, :], 0.25 * 1.5 ** 0.5)
            vec.memset(wc[:, :, G_ROWS:T_AT], 0.0)
            vec.tensor_copy(ident_b[:], a["ident"][:])
            vec.tensor_scalar_mul(vec_w[:], w2_in[:, 6, :, :], -0.25 * (1.5 ** 0.5) / 3.0).then_inc(vec_w_ready, 1)
            vec.tensor_scalar_mul(vec_w2[:], w2_in[:, 5, :, :], 0.25 * 3.0 ** -0.5).then_inc(vec_w2_ready, 1)
            dve.wait_ge(picks, 4 * SPLIT + 1)
            vec.tensor_copy(pick_b[:], pick_f[:])
            dve.wait_ge(vec_w_ready, 1)
            dve.wait_ge(vec_w2_ready, 1)
            vec.tensor_add(wv[:].rearrange("h (w u) -> h w u", u=MUL1), vec_w[:].rearrange("h u w -> h w u"),
                           vec_w2[:].rearrange("h u w -> h w u")).then_inc(weights_ready, 1)

            def tile_products(g, t):
                b = (g.base * T + t) % 2
                dve.wait_ge(xe_ready, g.times(T, t + 1))
                wait_count(dve, sgt_tile, g.times(T, t - 1))
                vec.tensor_mul(prod[b][:], p_xe[b][:].rearrange("p (i e) -> p i e", e=P),
                               spread(he[g.slot(UNROLL)][:, t * P:(t + 1) * P], [P, 4, P], 1)).then_inc(prod_ready, 1)
                dve.wait_ge(wv_ready, g.times(T, t + 1))
                if t == 0:
                    free(dve, redv_ready, g, 1)
                vec.tensor_mul(prodv[:, t, :].rearrange("p (k w u) -> p k w u", w=8, u=16),
                               spread(p_wv[b].rearrange("p (w u) -> p w u", u=16), [P, 3, 8, 16], 1),
                               spread(v16[g.slot(UNROLL)][:, t, :, :].rearrange("p u k -> p k u"), [P, 3, 8, 16], 2)).then_inc(wv_used, 1)

            def step(at):
                if g := at(1):
                    arrived(dve, loaded_a, g, LOADS_A)
                    wg.one_hot(dve, g)
                if g := at(3):
                    tile_products(g, 0)
                    tile_products(g, 1)
                if g := at(2):
                    s2 = g.slot(2)
                    done(dve, high_ready, g)
                    free(dve, low_ready, g, 2)
                    vec.tensor_sub(rest[s2][:], x32[s2][:], xs[s2][:, :, 0, :]).then_inc(rest_ready, 1)
                if g := at(4):
                    s, s2 = g.slot(UNROLL), g.slot(2)
                    done(dve, out_ready, g)
                    free(dve, vsum_ready, g, 1)
                    vec.tensor_mul(vout[:], spread(p_out[:, :, T_AT:SGT], [P, T, 8, 3], 3), spread(unit[s][:], [P, T, 8, 3], 2)).then_inc(vout_ready, 1)
                    free(dve, gate_copied, g, 2)
                    free(dve, msg_ready, g, 2)
                    vec.scalar_tensor_tensor(gate[s2][:], p_out[:, :, 0:G_ROWS], TANH_GAIN, spread(weight[s][:], [P, T, 16], 2),
                                             ALU.mult, ALU.mult).then_inc(gate_ready, 1)
                if g := at(3):
                    tile_products(g, 2)
                if g := at(4):
                    done(dve, redv_ready, g)
                    done(dve, vout_ready, g)
                    free(dve, msg_ready, g, 1)
                    vec.tensor_add(vsum[:], vout[:], redv[:].rearrange("p t (k w) -> p t w k", w=8)).then_inc(vsum_ready, 1)
                if g := at(2):
                    s2 = g.slot(2)
                    done(dve, mid_ready, g)
                    vec.tensor_sub(xs[s2][:, :, 2, :], rest[s2][:], xs[s2][:, :, 1, :]).then_inc(low_ready, 1)
                if g := at(3):
                    tile_products(g, 3)
                if g := at(4):
                    s2 = g.slot(2)
                    done(dve, vsum_ready, g)
                    done(dve, gate_ready, g)
                    free(dve, w.acc_ready, g, 2)
                    vec.tensor_mul(msg[s2][:, :, 8:32].rearrange("p t (w k) -> p t w k", k=3), vsum[:],
                                   spread(gate[s2][:, :, 8:16], [P, T, 8, 3], 3)).then_inc(msg_ready, 1)
                if g := at(3):
                    tile_products(g, 4)
                    dve.wait_ge(wv_used, g.times(T, T))
                    free(dve, vsum_ready, g, 1)
                    vec.tensor_reduce(redv[:], prodv[:].rearrange("p t (o u) -> p t o u", u=16), AX.X, ALU.add).then_inc(redv_ready, 1)
                if g := at(4):
                    w.add_window(dve, g)

            pipeline(dve, step)

        @block.scalar
        def _(act):
            def activate(g, t0, t1):
                act.wait_ge(sgt_tile, g.times(T, t1))
                to, at, n = sgt[g.slot(2)][:, t0 * P:t1 * P], t0 % 4 * P, (t1 - t0) * P
                nc.scalar.activation(to[0:G_ROWS, :], p_sgt[0:G_ROWS, at:at + n], ACT.Tanh, scale=1.0 / 32 ** 0.5)
                nc.scalar.copy(to[T_AT:SGT, :], p_sgt[T_AT:SGT, at:at + n]).then_inc(sgt_last if t1 == T else sgt_first, 1)

            act.wait_ge(sgt_zeroed, 2)

            def step(at):
                if g := at(4):
                    activate(g, 4, T)
                if g := at(2):
                    s2 = g.slot(2)
                    done(act, q_ready, g)
                    free(act, xt_mm, g, 2)
                    nc.scalar.copy(xs[s2][:, :, 0, :], x32[s2][:]).then_inc(high_ready, 1)
                if g := at(1):
                    s, s2 = g.slot(UNROLL), g.slot(2)
                    arrived(act, gathered, g, GATHERED)
                    free(act, low_ready, g, 2)
                    wait_count(act, wv_used, g.times(T, T - T * UNROLL))
                    nc.scalar.copy(x32[s2][:, :, 0:8], rows[s2][:, :, 0:8])
                    nc.scalar.copy(v16[s][:, :, 0:8, :].rearrange("p t u k -> p t (u k)"), rows[s2][:, :, 8:32]).then_inc(src_copied, 1)
                if g := at(4):
                    s2 = g.slot(2)
                    done(act, gate_ready, g)
                    free(act, w.acc_ready, g, 2)
                    nc.scalar.copy(msg[s2][:, :, 0:8], gate[s2][:, :, 0:8]).then_inc(gate_copied, 1)
                if g := at(2):
                    s2 = g.slot(2)
                    done(act, rest_ready, g)
                    nc.scalar.copy(xs[s2][:, :, 1, :], rest[s2][:]).then_inc(mid_ready, 1)
                if g := at(1):
                    s, s2 = g.slot(UNROLL), g.slot(2)
                    done(act, wg.rows_ready, g)
                    nc.scalar.copy(x32[s2][:, :, 8:16], p_rows[:, :, 0:8])
                    nc.scalar.copy(v16[s][:, :, 8:16, :].rearrange("p t u k -> p t (u k)"), p_rows[:, :, 8:32]).then_inc(dst_copied, 1)
                    done(act, he_mm, g)
                    wait_count(act, prod_ready, g.times(T, T - T * UNROLL))
                    wait_count(act, wv_ready, g.times(T, T - T * UNROLL))
                    nc.scalar.activation(he[s][:], p_he[:, 0:GE], ACT.Relu, scale=0.2 ** 0.5 / 4.0).then_inc(he_ready, 1)
                if g := at(3):
                    arrived(act, loaded_b, g, LOADS_B)
                    w.one_hot(act, g, negrel[g.slot(UNROLL)])
                if g := at(2):
                    done(act, xt_mm, g)
                    wait_count(act, xe_ready, g.times(T, -T))
                    nc.scalar.copy(xt[g.slot(2)][:], p_xt[:, 0:GE]).then_inc(xt_ready, 1)
                if g := at(3):
                    free(act, out_ready, g, 2)
                    activate(g, 0, 4)

            pipeline(act, step)

        @block.tensor
        def _(pe):
            def expand(g, t):
                b = (g.base * T + t) % 2
                wait_count(pe, prod_ready, g.times(T, t - 1))
                for i in range(4):
                    last = nc.tensor.matmul(p_xe[b][:, i * P:(i + 1) * P], pick_b[:, i, :], xt[g.slot(2)][:, t * P:(t + 1) * P],
                                            start=True, stop=True)
                last.then_inc(xe_ready, 1)
                wait_count(pe, wv_used, g.times(T, t - 1))
                nc.tensor.matmul(p_wv[b], he[g.slot(UNROLL)][0:HID1, t * P:(t + 1) * P], wv[:], start=True, stop=True
                                 ).then_inc(wv_ready, 1)

            def contract(g, t):
                b = (g.base * T + t) % 2
                pe.wait_ge(prod_ready, g.times(T, t + 1))
                if t == 0:
                    free(pe, sgt_last, g, 1)
                if t == 4:
                    done(pe, sgt_first, g)
                for i in range(4):
                    last = nc.tensor.matmul(p_sgt[:, t % 4 * P:(t % 4 + 1) * P], wc[:, i, :], prod[b][:, i, :], start=i == 0, stop=i == 3)
                last.then_inc(sgt_tile, 1)

            pe.wait_ge(weights_ready, 1)

            def step(at):
                if g := at(3):
                    done(pe, xt_ready, g)
                    done(pe, he_ready, g)
                    expand(g, 0)
                if g := at(4):
                    contract(g, 4)
                if g := at(3):
                    expand(g, 1)
                if g := at(4):
                    done(pe, sgt_last, g)
                    pe.wait_ge(dst_copied, g.times(1, 3) if at(2) else G)
                    free(pe, w.acc_added, g, 1)
                    for t in range(T):
                        last = nc.tensor.matmul(p_out[:, t, :], sgt[g.slot(2)][:, t * P:(t + 1) * P], a["ident"][0:SGT, 0:SGT],
                                                start=True, stop=True)
                    last.then_inc(out_ready, 1)
                if g := at(3):
                    contract(g, 0)
                    expand(g, 2)
                if g := at(1):
                    s = g.slot(UNROLL)
                    arrived(pe, loaded_a, g, LOADS_A)
                    free(pe, gate_ready, g, 3)
                    free(pe, vout_ready, g, 3)
                    free(pe, dst_copied, g, 1)
                    wg.product(pe, g)
                    free(pe, he_ready, g, 1)
                    free(pe, xt_ready, g, 2)
                    for c0, c1 in ((0, 512), (512, GE)):
                        last = nc.tensor.matmul(p_he[:, c0:c1], w1[:].rearrange("k u h -> k (u h)"), embt[s][:, c0:c1], start=True, stop=True)
                    last.then_inc(he_mm, 1)
                if g := at(3):
                    contract(g, 1)
                    expand(g, 3)
                    contract(g, 2)
                    expand(g, 4)
                    contract(g, 3)
                if g := at(2):
                    done(pe, low_ready, g)
                    free(pe, xt_ready, g, 1)
                    pe.wait_ge(he_ready, g.times(1, 2 if at(1) else 1))
                    for e in range(T):
                        last = nc.tensor.matmul(p_xt[:, e * P:(e + 1) * P], xs[g.slot(2)][:, e, :, :].rearrange("p s i -> p (s i)"),
                                                ident_b[:], start=True, stop=True)
                    last.then_inc(xt_mm, 1)
                if g := at(4):
                    done(pe, gate_copied, g)
                    pe.wait_ge(dst_copied, g.times(1, 4) if at(1) else G)
                    w.sum_window(pe, g, msg[g.slot(2)], msg_ready)

            pipeline(pe, step)


def window_pass_2(nc, a):
    LOADS, SCATTERED = 16 * 4, 16
    with ExitStack() as ctx:
        sem = a["sems"][2]
        sb, ps = tensors(nc, ctx, "w2")
        w = WindowGather(nc, a, 2, sb, ps)
        idx = [sb(f"idx{s}", [P, T], I32) for s in range(UNROLL)]
        row = [sb(f"row{s}", [P, T, P], I32) for s in range(UNROLL)]
        msg = [sb(f"msg{s}", [P, T, D]) for s in range(2)]
        summed = [sb(f"summed{s}", [P, T, D]) for s in range(4)]
        slot_idx = [sb(f"slot_idx{s}", [P, T], I32) for s in range(4)]
        same = [sb(f"same{s}", [P, T, P]) for s in range(2)]
        earlier = sb("earlier", [P, T, P])
        idxf = sb("idxf", [P, T])
        other = sb("other", [P, T])
        repeat = sb("repeat", [P, T])
        p_sum = ps("p_sum", [P, T, D])
        loaded = [sem(f"loaded{s}") for s in range(UNROLL)]
        scattered = [sem(f"scattered{t}") for t in range(T)]
        idxf_ready, same_ready, earlier_ready, repeat_ready, repeat1_ready, spare_ready, slot_ready = (
            sem(n) for n in ("idxf_ready", "same_ready", "earlier_ready", "repeat_ready", "repeat1_ready", "spare_ready", "slot_ready"))
        msg_ready, sum_ready, summed_ready = sem("msg_ready"), sem("sum_ready"), sem("summed_ready")

        def scatters_done(eng, g):
            for t in range(T):
                wait_count(eng, scattered[t], g.times(SCATTERED, -3 * SCATTERED))

        block = ctx.enter_context(nc.Block())

        @block.sync
        def _(sp):
            def step(at):
                if g := at(0):
                    s, k = g.slot(UNROLL), g.times(1)
                    free(sp, same_ready, g, UNROLL)
                    free(sp, w.rows_ready, g, UNROLL)
                    w.load(sp, g, loaded[s])
                    sp.dma_start(idx[s][:], pick(a["src"], k)).then_inc(loaded[s], 16)
                    sp.dma_start(row[s][:].rearrange("p t q -> p (t q)"),
                                 a["src_row"][bass.ds(k, 1), :].to_broadcast([P, GE])).then_inc(loaded[s], 16)

            pipeline(sp, step)

        @block.gpsimd
        def _(pool):
            def step(at):
                if g := at(3):
                    s4 = g.slot(4)
                    done(pool, slot_ready, g)
                    pool.nop(nofuse=True)
                    done(pool, summed_ready, g)
                    pool.nop(nofuse=True)
                    for t in range(T):
                        wait_count(pool, scattered[t], g.times(SCATTERED))
                        pool.nop(nofuse=True)
                        pool.indirect_dma_start(
                            out=a["acc"][2][t], out_offset=bass.IndirectOffsetOnAxis(ap=slot_idx[s4][:, t:t + 1], axis=0),
                            in_=summed[s4][:, t, :], in_offset=None, compute_op=ALU.add).then_inc(scattered[t], 16)

            pipeline(pool, step)
            for t in range(T):
                pool.wait_ge(scattered[t], SCATTERED * G)

        @block.vector
        def _(dve):
            vec = nc.vector

            def step(at):
                if g := at(1):
                    s, s2, s4 = g.slot(UNROLL), g.slot(2), g.slot(4)
                    arrived(dve, loaded, g, LOADS)
                    w.one_hot(dve, g)
                    free(dve, slot_ready, g, 1)
                    vec.tensor_copy(idxf[:], idx[s][:]).then_inc(idxf_ready, 1)
                    done(dve, idxf_ready, g)
                    free(dve, sum_ready, g, 2)
                    vec.tensor_tensor(same[s2][:], row[s][:], spread(idxf[:], [P, T, P], 2), ALU.is_equal).then_inc(same_ready, 1)
                    done(dve, same_ready, g)
                    vec.tensor_mul(earlier[:], same[s2][:], spread(a["before"][:], [P, T, P], 1)).then_inc(earlier_ready, 1)
                    vec.tensor_scalar(other[:], idxf[:], -1.0, a["trash"][:, 0:1], ALU.mult, ALU.add)
                    done(dve, earlier_ready, g)
                    vec.tensor_reduce(repeat[:], earlier[:], AX.X, ALU.add).then_inc(repeat_ready, 1)
                    done(dve, repeat_ready, g)
                    vec.tensor_scalar_min(repeat[:], repeat[:], 1.0).then_inc(repeat1_ready, 1)
                    done(dve, repeat1_ready, g)
                    vec.tensor_mul(other[:], repeat[:], other[:]).then_inc(spare_ready, 1)
                    done(dve, spare_ready, g)
                    scatters_done(dve, g)
                    vec.tensor_add(slot_idx[s4][:], idxf[:], other[:]).then_inc(slot_ready, 1)

            pipeline(dve, step)

        @block.tensor
        def _(pe):
            def step(at):
                if g := at(1):
                    arrived(pe, loaded, g, LOADS)
                    free(pe, msg_ready, g, 1)
                    w.product(pe, g)
                if g := at(2):
                    s2 = g.slot(2)
                    done(pe, same_ready, g)
                    done(pe, msg_ready, g)
                    free(pe, summed_ready, g, 1)
                    pe.nop(nofuse=True)
                    for t in range(T):
                        last = nc.tensor.matmul(p_sum[:, t, :], same[s2][:, t, :], msg[s2][:, t, :], start=True, stop=True)
                    last.then_inc(sum_ready, 1)

            pipeline(pe, step)

        @block.scalar
        def _(act):
            def step(at):
                if g := at(1):
                    done(act, w.rows_ready, g)
                    free(act, sum_ready, g, 2)
                    nc.scalar.copy(msg[g.slot(2)][:], w.p_rows).then_inc(msg_ready, 1)
                if g := at(2):
                    done(act, sum_ready, g)
                    scatters_done(act, g)
                    nc.scalar.copy(summed[g.slot(4)][:], p_sum[:]).then_inc(summed_ready, 1)

            pipeline(act, step)


def pick(table, at):
    return table[bass.ds(at, 1), :, :].rearrange("g p c -> (g p) c")


def build(nc, x, src, dst, src_row, dst_row, emb10, vec3, e32, e4, emb8, weight, eps, w1_1, w2_1, w2_uh, w1_3, w2_3, out):
    def dram(name, shape, dt=F32):
        return nc.dram_tensor(name, shape, dt, kind="Internal").ap()

    a = {
        "x": x, "src": src, "dst": dst, "src_row": src_row, "dst_row": dst_row, "e32": e32, "e4": e4,
        "weight": weight, "eps": eps, "w2_uh": w2_uh, "emb1": emb10, "emb3": emb8, "out": out,
        "w1_1": w1_1, "w2_1": w2_1, "w1_3": w1_3, "w2_3": w2_3, "unit_in": vec3,
        "table": [dram(f"table{i}", (N + WIN, D)) for i in range(4)],
        "acc": [[dram(f"acc{i}_{t}", (N + TRASH, D)) for t in range(T)] for i in range(4)],
        "deg": dram("deg", (HI * P, 1)),
    }
    a.update({
        "split": {layer: dram(f"split{layer}", (N + WIN, 3 * D), BF16) for layer in (1, 2)},
        "negrel": dram("negrel", (G, P, T)), "rel_row": dram("rel_row", (G, GE), BF16),
        "base": dram("base", (G, 1), I32), "span": dram("span", (G, 1)),
    })
    unit = dram("unit", (E, 3))
    a["unit"] = unit.rearrange("(p e) c -> p (e c)", p=NP)
    with ExitStack() as ctx:
        held = {
            "x_sb": ([NP, NJ * D], F32), "h_sb": ([NP, NJ * D], F32), "sums_sb": ([NP, NJ * D], F32), "norm_sb": ([NP, NJ], F32),
            "acc_t": ([D, N + WIN], F32), "base_sb": ([1, G], I32), "flag_sb": ([1, 1], I32),
            "row_iota": ([P, P], F32), "col_iota": ([P, 1], F32), "trash": ([P, 1], F32), "before": ([P, P], F32), "ident": ([P, P], F32),
        }
        for name, (shape, dt) in held.items():
            a[name] = ctx.enter_context(nc.sbuf_tensor(name, shape, dt))
        a["sems"] = [Sems(nc, f"edge{layer}") for layer in range(4)]
        setup_pass(nc, a)
        window_setup(nc, a)
        a["unit"] = unit.rearrange("(g p t) c -> g p (t c)", p=P, t=T)
        windowed = {0: window_pass_0, 1: window_pass_1, 2: window_pass_2, 3: window_pass_3}
        for layer in range(4):
            node_pass(nc, a, layer)
            fits = nc.values_load(a["flag_sb"][0:1, 0:1], min_val=0, max_val=1)
            with nc.If(fits == 1):
                windowed[layer](nc, a)
                if layer != 2:
                    window_sums(nc, a, layer)
            with nc.Else():
                if layer != 2:
                    clear_tables(nc, a, layer)
                edge_pass(nc, a, layer)
                if layer != 2:
                    table_sums(nc, a, layer)
            if layer == 2:
                table_sums(nc, a, layer)
            a["sems"][layer].clear()
        node_pass(nc, a, 4)


def kernel(x, src, dst, edge_attr_10, edge_attr_3, edge_attr_32, edge_attr_4, edge_attr_8, edge_weight,
           L0_gnn_eps, L1_gnn_W1, L1_gnn_W2, L3_gnn_fc_w1, L3_gnn_fc_w2):
    import numpy as np
    import concourse.bacc as bacc
    from concourse.bass_utils import run_bass_kernel_spmd

    c = np.ascontiguousarray

    def columns(z):
        return c(np.asarray(z).reshape(G, P, T, -1).transpose(0, 3, 2, 1).reshape(G, -1, GE))

    arrays = {
        "x": c(np.asarray(x).reshape(NP, NJ * D)),
        "src": c(np.asarray(src).reshape(G, P, T)),
        "dst": c(np.asarray(dst).reshape(G, P, T)),
        "src_row": columns(src).reshape(G, GE),
        "dst_row": columns(dst).reshape(G, GE),
        "emb10": columns(edge_attr_10),
        "vec3": c(np.asarray(edge_attr_3).reshape(NP, EJ * 3)),
        "e32": c(np.asarray(edge_attr_32).reshape(G, P, T * 32)),
        "e4": c(np.asarray(edge_attr_4).reshape(G, P, T * 4)),
        "emb8": columns(edge_attr_8),
        "weight": c(np.asarray(edge_weight).reshape(G, P, T)),
        "eps": c(np.broadcast_to(np.asarray(L0_gnn_eps).reshape(1, 1), (NP, 1))),
        "w1_1": c(np.asarray(L1_gnn_W1)),
        "w2_1": c(np.asarray(L1_gnn_W2).reshape(HID1, 7, MUL1, OUT1)),
        "w2_uh": c(np.asarray(L1_gnn_W2).reshape(HID1, 7, 2, 8, OUT1).transpose(3, 0, 2, 1, 4).reshape(P, 2, 7, OUT1)),
        "w1_3": c(np.asarray(L3_gnn_fc_w1)),
        "w2_3": c(np.asarray(L3_gnn_fc_w2).reshape(2, P, 4, MUL3, MUL3).transpose(1, 0, 2, 3, 4)),
    }
    nc = bacc.Bacc("TRN2", target_bir_lowering=False, num_devices=1)
    args = [nc.dram_tensor(name, z.shape, mybir.dt.from_np(z.dtype), kind="ExternalInput").ap() for name, z in arrays.items()]
    out = nc.dram_tensor("out", (NP, NJ * D), F32, kind="ExternalOutput").ap()
    build(nc, *args, out)
    r = run_bass_kernel_spmd(nc, [arrays], core_ids=[0])
    return r.results[0]["out"].reshape(N, D)
```
